# Optimizing a Trainium2 kernel written in Bass

```python
import numpy as np
import jax
import jax.numpy as jnp

def _softmax(x, axis=-1):
    return jax.nn.softmax(x, axis=axis)

def _gelu(x):
    return jax.nn.gelu(x, approximate=True)

def _silu(x):
    return jax.nn.silu(x)

def _sigmoid(x):
    return jax.nn.sigmoid(x)

def _layernorm(x, axis=-1, eps=1e-05):
    m = jnp.mean(x, axis=axis, keepdims=True)
    v = jnp.var(x, axis=axis, keepdims=True)
    return (x - m) / jnp.sqrt(v + eps)

def _scatter_add(tgt, idx, src, axis=0):
    return tgt.at[idx].add(src)

def _segment_sum(src, seg, n):
    return jax.ops.segment_sum(src, seg, n)
kernel_name = 'mk_adj_preln_d4_adj_r2_d8d8bf'

def setup_inputs(seed: int=0):
    np.random.seed(seed)
    _w = jnp.asarray

    def _rec_inputs():
        import jax
        import jax.numpy as jnp
        _gk = jax.random.key(seed)
        x = -1.394e-06 + 0.9999 * jax.random.normal(jax.random.fold_in(_gk, 1), (16, 512, 256), jnp.float32)
        _a = jax.random.bernoulli(jax.random.fold_in(_gk, 2), 0.03125, (16, 512, 512))
        adj = _a.astype(jnp.int32)
        return (x, adj)
    x, adj = _rec_inputs()

    def _L0_gnn_setup():
        import jax, jax.numpy as jnp
        import numpy as np
        NEG_INF = -1000000000.0
        NEG_SLOPE = 0.2

        def gat_layer(x, mask, W, a_src, a_dst, bias, concat):
            B, N, _ = x.shape
            H, F = a_src.shape
            xl = (x @ W).reshape(B, N, H, F)
            asrc = jnp.einsum('bnhf,hf->bnh', xl, a_src)
            adst = jnp.einsum('bnhf,hf->bnh', xl, a_dst)
            e = jax.nn.leaky_relu(asrc[:, :, None, :] + adst[:, None, :, :], NEG_SLOPE)
            e = jnp.where(mask[..., None], e, NEG_INF)
            attn = jax.nn.softmax(e, axis=1)
            out = jnp.einsum('bsdh,bshf->bdhf', attn, xl)
            if concat:
                out = out.reshape(B, N, H * F)
            else:
                out = out.mean(axis=2)
            return out + bias
        key = jax.random.key(seed)
        ks = jax.random.split(key, 10)
        B, N, Din, Fh, H, Dout = (8, 512, 256, 128, 4, 256)
        s = 0.05
        return {'adj': jax.random.randint(ks[0], (B, N, N), 0, 2, dtype=jnp.int32), 'x': jax.random.normal(ks[1], (B, N, Din), dtype=jnp.float32), 'W1': jax.random.normal(ks[2], (Din, H * Fh), dtype=jnp.float32) * s, 'att_src1': jax.random.normal(ks[3], (H, Fh), dtype=jnp.float32) * s, 'att_dst1': jax.random.normal(ks[4], (H, Fh), dtype=jnp.float32) * s, 'b1': jax.random.normal(ks[5], (H * Fh,), dtype=jnp.float32) * s, 'W2': jax.random.normal(ks[6], (H * Fh, Dout), dtype=jnp.float32) * s, 'att_src2': jax.random.normal(ks[7], (1, Dout), dtype=jnp.float32) * s, 'att_dst2': jax.random.normal(ks[8], (1, Dout), dtype=jnp.float32) * s, 'b2': jax.random.normal(ks[9], (Dout,), dtype=jnp.float32) * s}
    _L0_gnn_all = _L0_gnn_setup()
    _L0_gnn_in = {k: v for k, v in _L0_gnn_all.items() if k in ('W1', 'att_src1', 'att_dst1', 'b1', 'W2', 'att_src2', 'att_dst2', 'b2')}
    del _L0_gnn_all

    def _L1_gnn_setup():
        import jax, jax.numpy as jnp
        import numpy as np
        L = 3
        D = 256
        B, N = (8, 512)
        EPS = 1e-05

        def layernorm(x, gamma, beta):
            mu = jnp.mean(x, axis=-1, keepdims=True)
            var = jnp.var(x, axis=-1, keepdims=True)
            return (x - mu) * jax.lax.rsqrt(var + EPS) * gamma + beta
        key = jax.random.key(seed)
        ks = jax.random.split(key, 12)
        s = 1.0 / np.sqrt(D)
        node_features = jax.random.normal(ks[0], (B, N, D), dtype=jnp.float32)
        adjacency_matrix = jax.random.randint(ks[1], (B, N, N), 0, 2, dtype=jnp.int32)
        return {'node_features': node_features, 'adjacency_matrix': adjacency_matrix, 'attn_w': jax.random.normal(ks[2], (L, 2 * D), dtype=jnp.float32) * (1.0 / np.sqrt(2 * D)), 'attn_b': jax.random.normal(ks[3], (L,), dtype=jnp.float32) * 0.01, 'W1': jax.random.normal(ks[4], (L, D, 4 * D), dtype=jnp.float32) * s, 'b1': jnp.zeros((L, 4 * D), dtype=jnp.float32), 'W2': jax.random.normal(ks[5], (L, 4 * D, D), dtype=jnp.float32) * (1.0 / np.sqrt(4 * D)), 'b2': jnp.zeros((L, D), dtype=jnp.float32), 'g1': jnp.ones((L, D), dtype=jnp.float32), 'beta1': jnp.zeros((L, D), dtype=jnp.float32), 'g2': jnp.ones((L, D), dtype=jnp.float32), 'beta2': jnp.zeros((L, D), dtype=jnp.float32)}
    _L1_gnn_all = _L1_gnn_setup()
    _L1_gnn_in = {k: v for k, v in _L1_gnn_all.items() if k in ('attn_w', 'attn_b', 'W1', 'b1', 'W2', 'b2', 'g1', 'beta1', 'g2', 'beta2')}
    del _L1_gnn_all

    def _L2_gnn_setup():
        import jax, jax.numpy as jnp
        import numpy as np
        NEG_SLOPE = 0.2
        key = jax.random.key(seed)
        k1, k2, k3, k4, k5 = jax.random.split(key, 5)
        B, N, H = (8, 512, 256)
        node_features = jax.random.normal(k1, (B, N, H), dtype=jnp.float32)
        adjacency_matrix = jax.random.randint(k2, (B, N, N), 0, 2, dtype=jnp.int32)
        scale = 1.0 / np.sqrt(2 * H)
        attn_w_src = jax.random.uniform(k3, (H,), jnp.float32, -scale, scale)
        attn_w_dst = jax.random.uniform(k4, (H,), jnp.float32, -scale, scale)
        attn_b = jax.random.uniform(k5, (1,), jnp.float32, -scale, scale)
        return {'node_features': node_features, 'adjacency_matrix': adjacency_matrix, 'attn_w_src': attn_w_src, 'attn_w_dst': attn_w_dst, 'attn_b': attn_b}
    _L2_gnn_all = _L2_gnn_setup()
    _L2_gnn_in = {k: v for k, v in _L2_gnn_all.items() if k in ('attn_w_src', 'attn_w_dst', 'attn_b')}
    del _L2_gnn_all

    def _L3_gnn_setup():
        import jax, jax.numpy as jnp
        import numpy as np
        B, N, DIN, DOUT = (8, 1024, 256, 256)
        key = jax.random.key(seed)
        kx, ka, kw, kb, kattn = jax.random.split(key, 5)
        x = jax.random.normal(kx, (B, N, DIN), dtype=jnp.float32)
        adjacency_matrix = jax.random.randint(ka, (B, N, N), 0, 2, dtype=jnp.int32)
        lim_w = float(np.sqrt(1.0 / DIN))
        W = jax.random.uniform(kw, (DOUT, DIN), minval=-lim_w, maxval=lim_w, dtype=jnp.float32)
        b = jax.random.uniform(kb, (DOUT,), minval=-lim_w, maxval=lim_w, dtype=jnp.float32)
        lim_a = float(np.sqrt(6.0 / (DOUT + DOUT)))
        attn = jax.random.uniform(kattn, (DOUT, DOUT), minval=-lim_a, maxval=lim_a, dtype=jnp.float32)
        return {'x': x, 'adjacency_matrix': adjacency_matrix, 'W': W, 'b': b, 'attn': attn}
    _L3_gnn_all = _L3_gnn_setup()
    _L3_gnn_in = {k: v for k, v in _L3_gnn_all.items() if k in ('W', 'b', 'attn')}
    del _L3_gnn_all
    return {'x': x, 'adj': adj, 'L0_gnn_W1': _L0_gnn_in['W1'], 'L0_gnn_att_src1': _L0_gnn_in['att_src1'], 'L0_gnn_att_dst1': _L0_gnn_in['att_dst1'], 'L0_gnn_b1': _L0_gnn_in['b1'], 'L0_gnn_W2': _L0_gnn_in['W2'], 'L0_gnn_att_src2': _L0_gnn_in['att_src2'], 'L0_gnn_att_dst2': _L0_gnn_in['att_dst2'], 'L0_gnn_b2': _L0_gnn_in['b2'], 'L1_gnn_attn_w': _L1_gnn_in['attn_w'], 'L1_gnn_attn_b': _L1_gnn_in['attn_b'], 'L1_gnn_W1': _L1_gnn_in['W1'], 'L1_gnn_b1': _L1_gnn_in['b1'], 'L1_gnn_W2': _L1_gnn_in['W2'], 'L1_gnn_b2': _L1_gnn_in['b2'], 'L1_gnn_g1': _L1_gnn_in['g1'], 'L1_gnn_beta1': _L1_gnn_in['beta1'], 'L1_gnn_g2': _L1_gnn_in['g2'], 'L1_gnn_beta2': _L1_gnn_in['beta2'], 'L2_gnn_attn_w_src': _L2_gnn_in['attn_w_src'], 'L2_gnn_attn_w_dst': _L2_gnn_in['attn_w_dst'], 'L2_gnn_attn_b': _L2_gnn_in['attn_b'], 'L3_gnn_W': _L3_gnn_in['W'], 'L3_gnn_b': _L3_gnn_in['b'], 'L3_gnn_attn': _L3_gnn_in['attn']}

def reference(x, adj, L0_gnn_W1, L0_gnn_att_src1, L0_gnn_att_dst1, L0_gnn_b1, L0_gnn_W2, L0_gnn_att_src2, L0_gnn_att_dst2, L0_gnn_b2, L1_gnn_attn_w, L1_gnn_attn_b, L1_gnn_W1, L1_gnn_b1, L1_gnn_W2, L1_gnn_b2, L1_gnn_g1, L1_gnn_beta1, L1_gnn_g2, L1_gnn_beta2, L2_gnn_attn_w_src, L2_gnn_attn_w_dst, L2_gnn_attn_b, L3_gnn_W, L3_gnn_b, L3_gnn_attn):
    import jax
    import jax.numpy as jnp

    def _L0_gnn_ref(adj, x, W1, att_src1, att_dst1, b1, W2, att_src2, att_dst2, b2):
        import jax, jax.numpy as jnp
        import numpy as np
        NEG_INF = -1000000000.0
        NEG_SLOPE = 0.2

        def gat_layer(x, mask, W, a_src, a_dst, bias, concat):
            B, N, _ = x.shape
            H, F = a_src.shape
            xl = (x @ W).reshape(B, N, H, F)
            asrc = jnp.einsum('bnhf,hf->bnh', xl, a_src)
            adst = jnp.einsum('bnhf,hf->bnh', xl, a_dst)
            e = jax.nn.leaky_relu(asrc[:, :, None, :] + adst[:, None, :, :], NEG_SLOPE)
            e = jnp.where(mask[..., None], e, NEG_INF)
            attn = jax.nn.softmax(e, axis=1)
            out = jnp.einsum('bsdh,bshf->bdhf', attn, xl)
            if concat:
                out = out.reshape(B, N, H * F)
            else:
                out = out.mean(axis=2)
            return out + bias
        B, N, _ = adj.shape
        mask = (adj > 0) | jnp.eye(N, dtype=bool)[None]
        h = jax.nn.elu(gat_layer(x, mask, W1, att_src1, att_dst1, b1, concat=True))
        h = gat_layer(h, mask, W2, att_src2, att_dst2, b2, concat=False)
        return h

    def _L1_gnn_ref(node_features, adjacency_matrix, attn_w, attn_b, W1, b1, W2, b2, g1, beta1, g2, beta2):
        import jax, jax.numpy as jnp
        import numpy as np
        L = 3
        D = 256
        B, N = (8, 512)
        EPS = 1e-05

        def layernorm(x, gamma, beta):
            mu = jnp.mean(x, axis=-1, keepdims=True)
            var = jnp.var(x, axis=-1, keepdims=True)
            return (x - mu) * jax.lax.rsqrt(var + EPS) * gamma + beta
        n = adjacency_matrix.shape[-1]
        mask = adjacency_matrix.astype(jnp.float32) + jnp.eye(n, dtype=jnp.float32) > 0
        x = node_features
        d = x.shape[-1]
        for l in range(attn_w.shape[0]):
            si = x @ attn_w[l, :d]
            sj = x @ attn_w[l, d:]
            scores = si[:, :, None] + sj[:, None, :] + attn_b[l]
            scores = jnp.where(scores >= 0, scores, 0.2 * scores)
            scores = jnp.where(mask, scores, -jnp.inf)
            attn = jax.nn.softmax(scores, axis=-1)
            agg = jnp.einsum('bij,bjd->bid', attn, x)
            h = layernorm(x + agg, g1[l], beta1[l])
            ff = jax.nn.gelu(h @ W1[l] + b1[l], approximate=False) @ W2[l] + b2[l]
            x = layernorm(h + ff, g2[l], beta2[l])
        return x

    def _L2_gnn_ref(node_features, adjacency_matrix, attn_w_src, attn_w_dst, attn_b):
        import jax, jax.numpy as jnp
        import numpy as np
        NEG_SLOPE = 0.2
        B, N, H = node_features.shape
        s_src = jnp.einsum('bnh,h->bn', node_features, attn_w_src)
        s_dst = jnp.einsum('bnh,h->bn', node_features, attn_w_dst)
        scores = s_src[:, :, None] + s_dst[:, None, :] + attn_b[0]
        scores = jax.nn.leaky_relu(scores, negative_slope=NEG_SLOPE)
        adj = adjacency_matrix.astype(jnp.float32) + jnp.eye(N, dtype=jnp.float32)[None]
        scores = jnp.where(adj == 0, -jnp.inf, scores)
        attn = jax.nn.softmax(scores, axis=-1)
        return jnp.einsum('bij,bjh->bih', attn, node_features)

    def _L3_gnn_ref(x, adjacency_matrix, W, b, attn):
        import jax, jax.numpy as jnp
        import numpy as np
        B, N, DIN, DOUT = (8, 1024, 256, 256)
        h = jnp.einsum('bni,oi->bno', x, W) + b
        ha = jnp.einsum('bmi,ij->bmj', h, attn)
        scores = jnp.einsum('bmj,bnj->bmn', ha, h)
        scores = jnp.where(adjacency_matrix == 0, -jnp.inf, scores)
        attn_weights = jax.nn.softmax(scores, axis=-1)
        x_out = jnp.einsum('bmn,bnd->bmd', attn_weights, h)
        return jax.nn.elu(x_out)
    h = jnp.maximum(_layernorm(x, axis=-1), 0.0)
    x = x + _L0_gnn_ref(adj, h, L0_gnn_W1, L0_gnn_att_src1, L0_gnn_att_dst1, L0_gnn_b1, L0_gnn_W2, L0_gnn_att_src2, L0_gnn_att_dst2, L0_gnn_b2)
    h = jnp.maximum(_layernorm(x, axis=-1), 0.0)
    x = x + _L1_gnn_ref(h, adj, L1_gnn_attn_w, L1_gnn_attn_b, L1_gnn_W1, L1_gnn_b1, L1_gnn_W2, L1_gnn_b2, L1_gnn_g1, L1_gnn_beta1, L1_gnn_g2, L1_gnn_beta2)
    h = jnp.maximum(_layernorm(x, axis=-1), 0.0)
    x = x + _L2_gnn_ref(h, adj, L2_gnn_attn_w_src, L2_gnn_attn_w_dst, L2_gnn_attn_b)
    h = jnp.maximum(_layernorm(x, axis=-1), 0.0)
    x = x + _L3_gnn_ref(h, adj, L3_gnn_W, L3_gnn_b, L3_gnn_attn)
    return x

_drawn_inputs = setup_inputs


def setup_inputs(seed=0):
    import zlib

    import numpy as np

    out = dict(_drawn_inputs(seed))
    spreads = {'L1_gnn_b1': (0.0, 0.1),
     'L1_gnn_b2': (0.0, 0.1),
     'L1_gnn_g1': (1.0, 0.2),
     'L1_gnn_beta1': (0.0, 0.1),
     'L1_gnn_g2': (1.0, 0.2),
     'L1_gnn_beta2': (0.0, 0.1)}
    factors = {'L0_gnn_att_src1': 3.314,
     'L0_gnn_att_dst1': 100.829,
     'L0_gnn_att_src2': 8.0,
     'L0_gnn_att_dst2': 200.0,
     'L1_gnn_attn_b': 200.0,
     'L2_gnn_attn_w_src': 8.0,
     'L2_gnn_attn_w_dst': 8.0,
     'L3_gnn_b': 3.484}
    for name, (base, spread) in spreads.items():
        noise = np.random.default_rng([zlib.crc32(name.encode()), seed]).standard_normal(out[name].shape)
        drawn = base * np.exp(spread * noise) if base else spread * noise
        out[name] = jnp.asarray(drawn.astype(out[name].dtype))
    for name, factor in factors.items():
        out[name] = (out[name] * factor).astype(out[name].dtype)
    return out
```

```python
from contextlib import ExitStack

import concourse.bass as bass
from concourse import mybir

ALU = mybir.AluOpType
ACT = mybir.ActivationFunctionType
F32 = mybir.dt.float32
BF16 = mybir.dt.bfloat16
I32 = mybir.dt.int32

P = 128
UNITS = 2
BANKS = 4
BIG = 1e30
SLOPE = 0.2
EPS = 1e-5
HEADS = 4
ATT_L1, ATT_L2 = HEADS + 1, HEADS + 4


def steps_of(u):
    s = [("load", u, 0), ("mask", u, 0), ("norm", u, 0), ("turn", u, 0), ("proj1", u, 0), ("max", u, 0)]
    for h in range(HEADS):
        s.append(("weights", u, h))
        if h + 1 < HEADS:
            s.append(("max", u, h + 1))
        s.append(("gather", u, h))
    s += [("elu", u, 0), ("turn1", u, 0), ("proj2", u, 0)]
    s += [("max", u, HEADS), ("weights", u, HEADS), ("gather", u, HEADS)]
    s.append(("norm", u, 1))
    for l in range(3):
        a = ATT_L1 + l
        s += [("score", u, l), ("max", u, a), ("weights", u, a), ("gather", u, a), ("affine", u, 2 * l),
              ("turn", u, 1 + l), ("ffn", u, l), ("affine", u, 2 * l + 1)]
    s += [("resid", u, 0), ("norm", u, 2), ("score", u, 3)]
    s += [("max", u, ATT_L2), ("weights", u, ATT_L2), ("gather", u, ATT_L2)]
    s += [("norm", u, 3), ("turn", u, 4), ("dotproj", u, 0), ("dotscore", u, 0), ("dotturn", u, 0),
          ("dotout", u, 0), ("store", u, 0)]
    return s


def interleave():
    lists = [steps_of(u) for u in range(UNITS)]
    return [s for group in zip(*lists) for s in group]


STEPS = interleave()


def plan(T, KC, FC):
    groups, marks = [], {}

    def mark(name, *keys):
        marks.setdefault(name, []).extend(keys)

    for name, u, n in STEPS:
        if name == "mask":
            mark("edges", u)
            mark("masks", u)
            groups += [("maskT", u, c) for c in range(T)]
        elif name == "norm":
            mark("moments", (u, "n", n))
            mark("rstd", (u, "n", n))
            mark("normed", (u, n))
            if n == 0:
                mark("xbias", u)
        elif name == "affine":
            mark("moments", (u, "a", n))
            mark("rstd", (u, "a", n))
            mark("layered", (u, n))
        elif name == "turn":
            groups += [("turn", u, n, c) for c in range(KC)]
            if 1 <= n <= 3:
                mark("hbias", (u, n - 1))
        elif name == "proj1":
            groups += [("cols1", u)] + [("values1", u, t) for t in range(T)]
            mark("ones1", u)
        elif name == "proj2":
            groups += [("cols2", u)] + [("values2", u, t) for t in range(T)]
        elif name == "score":
            mark("cols", (u, n))
        elif name == "max":
            groups.append(("arow", u, n))
            mark("shift", (u, n))
        elif name == "weights":
            mark("rows", (u, n, 2), (u, n, 1))
            for t in range(T):
                mark("low", (u, n, t))
                mark("high", (u, n, t))
                mark("masked", (u, n, t))
                mark("exp", (u, n, t))
        elif name == "gather":
            groups += [("gather", u, n, t) for t in range(T)]
        elif name == "elu":
            mark("elu_exp", *[(u, t) for t in range(T)])
            mark("elu", *[(u, t) for t in range(T)])
        elif name == "turn1":
            groups += [("turn1", u, c) for c in range(T)]
        elif name == "ffn":
            groups += [("up", u, n, f) for f in range(FC)] + [("down", u, n, t) for t in range(T)]
        elif name == "resid":
            mark("summed", u)
        elif name == "dotproj":
            groups += [("hT", u, c) for c in range(KC)] + [("h", u, t) for t in range(T)]
            groups += [("haT", u, c) for c in range(KC)]
        elif name == "dotscore":
            groups += [("dots", u, t) for t in range(T)]
            mark("dotmax", u)
            mark("dotexp", u)
        elif name == "dotturn":
            groups += [("probT", u, t) for t in range(T)]
        elif name == "dotout":
            groups += [("dotout", u, t) for t in range(T)]
            mark("out_exp", *[(u, t) for t in range(T)])
            mark("out", u)
    return groups, marks


def gnn_kernel(nc, x, adj, w1, as1, ad1, b1, w2, as2, ad2, b2, aw, ab, fw1, fb1, fw2, fb2, g1, be1, g2, be2,
               sw, dw, sb2, w3t, b3, attn3, b3_by_part, out):
    B, N, D = x.shape
    T = N // P
    KC = D // P
    HF = w1.shape[1] // HEADS
    D1 = HEADS * HF
    LAYERS, _, FF = fw1.shape
    FC = FF // P
    TURNS = B // UNITS
    assert HF == P and D1 == N and T == HEADS and FC == 2 * T

    groups, marks = plan(T, KC, FC)
    group_at = {g: i for i, g in enumerate(groups)}
    mark_at = {name: {k: i for i, k in enumerate(keys)} for name, keys in marks.items()}
    uses_of_bank = [len(range(b, len(groups), BANKS)) for b in range(BANKS)]

    with ExitStack() as ctx:
        def sb(name, shape, dt=F32):
            return ctx.enter_context(nc.sbuf_tensor(name, shape, dt))

        def sem(name):
            return ctx.enter_context(nc.semaphore(name))

        W1 = sb("W1", [P, KC, D1])
        W2 = sb("W2", [P, T, D])
        FW1 = sb("FW1", [P, LAYERS, KC, FF])
        FW2 = sb("FW2", [P, LAYERS, FC, D])
        W3T = sb("W3T", [P, KC, D])
        A3 = sb("A3", [P, KC, D])
        b1row = sb("b1row", [P, D1])
        b2row = sb("b2row", [P, D])
        g_row = sb("g_row", [P, 2 * LAYERS, D])
        be_row = sb("be_row", [P, 2 * LAYERS, D])
        fb2row = sb("fb2row", [P, LAYERS, D])
        s_row = sb("s_row", [P, LAYERS + 1, 2, D])
        s_bias = sb("s_bias", [P, LAYERS + 1])
        b3row = sb("b3row", [P, D])
        fb1col = sb("fb1col", [P, LAYERS, FC])
        b3col = sb("b3col", [P, KC])
        wa1 = sb("wa1", [P, KC, 2 * HEADS])
        wa2 = sb("wa2", [P, T, 2])
        ident = sb("ident", [P, P])
        identb = sb("identb", [P, P], BF16)
        offdiag = sb("offdiag", [P, P], BF16)
        c_eps = sb("c_eps", [P, T])
        c_neg1 = sb("c_neg1", [P, T])
        c_half = sb("c_half", [P, T])
        gate = sb("gate", [P, 64])
        junk = sb("junk", [P, T, N], BF16)
        edges = sb("edges", [P, T, N], I32)

        def per_unit(name, shape, dt=F32):
            return [sb(f"{name}{u}", shape, dt) for u in range(UNITS)]

        X = per_unit("X", [P, T, D])
        HX = per_unit("HX", [P, T, D + 1])
        HT = per_unit("HT", [P, KC, N])
        M3 = per_unit("M3", [P, T, N], BF16)
        MN = per_unit("MN", [P, T, N], BF16)
        MT = per_unit("MT", [P, T, N], BF16)
        LOW = per_unit("LOW", [P, 2, N])
        Z = per_unit("Z", [P, T, N])
        G = per_unit("G", [P, T, N])
        V1 = per_unit("V1", [P, T, HEADS * (HF + 1)])
        ab1 = per_unit("ab1", [P, T, 2 * HEADS])
        ab2 = per_unit("ab2", [P, T, 2])
        cols = per_unit("cols", [P, 2, 5, T])
        a_low = per_unit("a_low", [P, 2, T])
        stats = per_unit("stats", [P, T, 6])
        mv = per_unit("mv", [P, T, 2])
        norm_c = per_unit("norm_c", [P, 4, T])
        rden = per_unit("rden", [P, T])
        dmax = per_unit("dmax", [P, 4, T])
        dden = per_unit("dden", [P, T])

        ring = [ctx.enter_context(nc.psum_tensor(f"ring{b}", [P, N], F32)) for b in range(BANKS)]
        row_hi = [ctx.enter_context(nc.psum_tensor(f"row_hi{u}", [P, N], F32)) for u in range(UNITS)]
        row_lo = [ctx.enter_context(nc.psum_tensor(f"row_lo{u}", [P, N], F32)) for u in range(UNITS)]

        s_w = sem("weights_loaded")
        s_const = sem("constants_set")
        s_fold = sem("score_weights_folded")
        s_x = [sem(f"x_loaded{u}") for u in range(UNITS)]
        s_adj = sem("adj_loaded")
        s_store = [sem(f"stored{u}") for u in range(UNITS)]
        s_mm = sem("product_done")
        s_free = [sem(f"bank_read{b}") for b in range(BANKS)]
        s_dve = sem("vector_step")
        s_pool = sem("pool_step")
        S = {name: sem(f"{name}_done") for name in marks}

        SEED = 1

        def bank(key):
            return ring[group_at[key] % BANKS]

        def freed(key):
            return s_free[group_at[key] % BANKS]

        def product(it, key):
            return it * len(groups) + group_at[key] + 1

        def readout(it, key):
            g = group_at[key]
            return SEED + it * uses_of_bank[g % BANKS] + g // BANKS + 1

        def done(it, name, key):
            return (SEED if name == "edges" else 0) + it * len(marks[name]) + mark_at[name][key] + 1

        def V1h(u, t, h):
            return V1[u][:, t, h * (HF + 1):(h + 1) * (HF + 1)]

        def H1T(u, c):
            return V1[u][:, :, :].rearrange("p t n -> p (t n)")[:, c * N:(c + 1) * N]

        def hidden(u, f):
            return G[u][:, f, :] if f < T else H1T(u, f - T)

        def R1(u, t):
            return G[u][:, :, :].rearrange("p t n -> p (t n)")[:, t * D:(t + 1) * D]

        def a_cols(u, n):
            return ab1[u][:, :, n] if n < HEADS else ab2[u][:, :, 0]

        def b_cols(u, n):
            return ab1[u][:, :, HEADS + n] if n < HEADS else ab2[u][:, :, 1]

        def masks(u, n):
            return (MN[u], MT[u]) if n <= HEADS else (MT[u], MN[u])

        def values(u, n, t):
            return V1h(u, t, n) if n < HEADS else HX[u][:, t, :]

        nodes = "b (t p) d -> b p t d"
        x_v, adj_v, out_v = (a.rearrange(nodes, p=P) for a in (x, adj, out))

        block = ctx.enter_context(nc.Block())
        loads = [
            (W1[:, :, :], w1.rearrange("(k p) n -> p k n", p=P)),
            (W2[:, :, :], w2.rearrange("(k p) n -> p k n", p=P)),
            (W3T[:, :, :], w3t.rearrange("(k p) n -> p k n", p=P)),
            (A3[:, :, :], attn3.rearrange("(k p) n -> p k n", p=P)),
            (b1row[:, :], b1.partition_broadcast(P)),
            (b2row[:, :], b2.partition_broadcast(P)),
            (b3row[:, :], b3.partition_broadcast(P)),
            (fb1col[:, :, :], fb1),
            (b3col[:, :], b3_by_part),
            (fb2row[:, :, :], fb2.partition_broadcast(P)),
            (s_row[:, LAYERS, 0, :], dw.partition_broadcast(P)),
            (s_row[:, LAYERS, 1, :], sw.partition_broadcast(P)),
            (s_bias[:, 0:LAYERS], ab.partition_broadcast(P)),
            (s_bias[:, LAYERS:LAYERS + 1], sb2.partition_broadcast(P)),
            (G[0][:, 0, :], as1.rearrange("h f -> (h f)").partition_broadcast(P)),
            (G[0][:, 1, :], ad1.rearrange("h f -> (h f)").partition_broadcast(P)),
            (G[0][:, 2, 0:D], as2.rearrange("h f -> (h f)").partition_broadcast(P)),
            (G[0][:, 2, D:2 * D], ad2.rearrange("h f -> (h f)").partition_broadcast(P)),
        ]
        for l in range(LAYERS):
            loads += [
                (FW1[:, l, :, :], fw1[l].rearrange("(k p) n -> p k n", p=P)),
                (FW2[:, l, :, :], fw2[l].rearrange("(k p) n -> p k n", p=P)),
                (g_row[:, 2 * l, :], g1[l].partition_broadcast(P)),
                (g_row[:, 2 * l + 1, :], g2[l].partition_broadcast(P)),
                (be_row[:, 2 * l, :], be1[l].partition_broadcast(P)),
                (be_row[:, 2 * l + 1, :], be2[l].partition_broadcast(P)),
                (s_row[:, l, 1, :], aw[l, 0:D].partition_broadcast(P)),
                (s_row[:, l, 0, :], aw[l, D:2 * D].partition_broadcast(P)),
            ]

        @block.sync
        def _(sp):
            for free in s_free:
                sp.sem_inc(free, SEED)
            sp.sem_inc(S["edges"], SEED)
            for u in range(UNITS):
                sp.sem_inc(s_store[u], 16 * SEED)
            for dst, src in loads:
                sp.dma_start(dst, src).then_inc(s_w, 16)
            with sp.Fori(0, TURNS) as it:
                for name, u, n in STEPS:
                    if name == "load":
                        sp.wait_ge(s_store[u], 16 * SEED + it * 16)
                        sp.dma_start(X[u][:, :, :], x_v[it * UNITS + u]).then_inc(s_x[u], 16)
                        sp.wait_ge(S["edges"], SEED + it * UNITS + u)
                        sp.dma_start(edges[:, :, :], adj_v[it * UNITS + u]).then_inc(s_adj, 16)
                    elif name == "store":
                        sp.wait_ge(S["out"], done(it, "out", u))
                        sp.dma_start(out_v[it * UNITS + u], X[u][:, :, :]).then_inc(s_store[u], 16)
            for u in range(UNITS):
                sp.wait_ge(s_store[u], 16 * SEED + 16 * TURNS)

        @block.gpsimd
        def _(pool):
            pool.memset(ident[:, :], 0.0)
            pool.memset(identb[:, :], 0.0)
            pool.memset(offdiag[:, :], 1.0)
            pool.memset(c_eps[:, :], EPS)
            pool.memset(c_neg1[:, :], -1.0)
            for u in range(UNITS):
                pool.memset(HX[u][:, :, D:D + 1], 1.0)
            pool.memset(c_half[:, :], -0.5).then_inc(s_const, 1)
            pool.wait_ge(s_const, 1)
            for m, v in ((ident, 1.0), (identb, 1.0), (offdiag, 0.0)):
                pool.affine_select(out=m[:, :], in_=m[:, :], compare_op=ALU.not_equal, fill=v, base=0,
                                   pattern=[[-1, P]], channel_multiplier=1).then_inc(s_const, 1)
            pool.wait_ge(s_const, 4)
            pool.wait_ge(s_w, 16 * len(loads))
            links = [0]
            with pool.Fori(0, TURNS) as it:
                def link(ins):
                    links[0] += 1
                    ins.then_inc(s_pool, 1)
                    pool.wait_ge(s_pool, it * POOL_LINKS + links[0])

                POOL_LINKS = UNITS * (1 + 2 * (4 + 2 * LAYERS))
                for name, u, n in STEPS:
                    if name == "mask":
                        pool.wait_ge(S["edges"], done(it, "edges", u))
                        for t in range(T):
                            d = MN[u][:, t, t * P:(t + 1) * P]
                            pool.tensor_tensor(d, d, offdiag[:, :], ALU.mult)
                        for t in range(T):
                            pool.wait_ge(freed(("maskT", u, t)), readout(it, ("maskT", u, t)))
                            d = MT[u][:, t, t * P:(t + 1) * P]
                            ins = pool.tensor_tensor(d, d, offdiag[:, :], ALU.mult)
                        ins.then_inc(S["masks"], 1)
                    elif name in ("norm", "affine"):
                        key = (u, name[0], n)
                        pool.wait_ge(S["moments"], done(it, "moments", key))
                        c = norm_c[u]
                        pool.tensor_tensor(c[:, 2, :], mv[u][:, :, 0], c_neg1[:, :], ALU.mult)
                        link(pool.tensor_tensor(c[:, 0, :], mv[u][:, :, 1], c_eps[:, :], ALU.add))
                        link(pool.tensor_tensor(c[:, 1, :], c[:, 0, :], c_half[:, :], ALU.pow))
                        pool.tensor_tensor(c[:, 3, :], c[:, 2, :], c[:, 1, :], ALU.mult).then_inc(S["rstd"], 1)
                        if name == "norm" and n == 0:
                            pool.wait_ge(S["normed"], done(it, "normed", (u, 0)))
                            for t in range(T):
                                ins = pool.tensor_tensor(X[u][:, t, :], X[u][:, t, :], b2row[:, :], ALU.add)
                            ins.then_inc(S["xbias"], 1)
                    elif name == "proj1":
                        ones = V1[u][:, :, :].rearrange("p t (h f) -> p t h f", h=HEADS)[:, :, :, HF]
                        pool.memset(ones, 1.0).then_inc(S["ones1"], 1)
                    elif name == "turn" and 1 <= n <= LAYERS:
                        pool.wait_ge(s_mm, product(it, ("turn", u, n, KC - 1)))
                        for t in range(T):
                            ins = pool.tensor_tensor(HX[u][:, t, 0:D], HX[u][:, t, 0:D], fb2row[:, n - 1, :],
                                                     ALU.add)
                        ins.then_inc(S["hbias"], 1)
                    elif name == "weights":
                        for t in range(T):
                            pool.wait_ge(S["high"], done(it, "high", (u, n, t)))
                            pool.tensor_tensor(Z[u][:, t, :], Z[u][:, t, :], masks(u, n)[0][:, t, :],
                                               ALU.add).then_inc(S["masked"], 1)
                    elif name == "resid":
                        pool.wait_ge(S["layered"], done(it, "layered", (u, 2 * LAYERS - 1)))
                        link(pool.tensor_tensor(X[u][:, 0:T // 2, :], X[u][:, 0:T // 2, :],
                                                HX[u][:, 0:T // 2, 0:D], ALU.add))
                        pool.tensor_tensor(X[u][:, T // 2:T, :], X[u][:, T // 2:T, :],
                                           HX[u][:, T // 2:T, 0:D], ALU.add).then_inc(S["summed"], 1)
                assert links[0] == POOL_LINKS, links[0]

        @block.scalar
        def _(act):
            act.wait_ge(s_w, 16 * len(loads))
            with act.Fori(0, TURNS) as it:
                def read(dst, src_of, key, func=ACT.Copy, **kw):
                    act.wait_ge(s_mm, product(it, key))
                    act.activation(dst, src_of(bank(key)), func, **kw).then_inc(freed(key), 1)

                for name, u, n in STEPS:
                    if name == "mask":
                        for c in range(T):
                            read(MT[u][:, c, :], lambda b: b[:, :].bitcast(BF16)[:, 0:N], ("maskT", u, c))
                    elif name == "norm":
                        act.wait_ge(S["rstd"], done(it, "rstd", (u, "n", n)))
                        for t in range(T):
                            ins = act.activation(HX[u][:, t, 0:D], X[u][:, t, :], ACT.Relu,
                                                 bias=norm_c[u][:, 3, t:t + 1], scale=norm_c[u][:, 1, t:t + 1])
                        ins.then_inc(S["normed"], 1)
                    elif name == "turn":
                        for c in range(KC):
                            read(HT[u][:, c, :], lambda b: b[:, :], ("turn", u, n, c))
                    elif name == "proj1":
                        act.wait_ge(S["ones1"], done(it, "ones1", u))
                        for t in range(T):
                            v = V1[u][:, t, :].rearrange("p (h f) -> p h f", h=HEADS)[:, :, 0:HF]
                            read(v, lambda b: b[:, :].rearrange("p (h f) -> p h f", h=HEADS), ("values1", u, t))
                    elif name == "proj2":
                        for t in range(T):
                            read(HX[u][:, t, 0:D], lambda b: b[:, 0:D], ("values2", u, t))
                    elif name == "weights":
                        def low(t):
                            if t == 0:
                                act.wait_ge(S["rows"], done(it, "rows", (u, n, 2)))
                            if t >= 2:
                                act.wait_ge(S["high"], done(it, "high", (u, n, t - 2)))
                            act.activation(LOW[u][:, t % 2, :], row_lo[u][:, :], ACT.Identity,
                                           bias=a_low[u][:, n % 2, t:t + 1]).then_inc(S["low"], 1)

                        def exp(t):
                            act.wait_ge(S["masked"], done(it, "masked", (u, n, t)))
                            act.activation(Z[u][:, t, :], Z[u][:, t, :], ACT.Exp).then_inc(S["exp"], 1)

                        low(0)
                        low(1)
                        for t in range(2, T):
                            low(t)
                            exp(t - 2)
                        exp(T - 2)
                        exp(T - 1)
                    elif name == "elu":
                        for t in range(T):
                            if t == 0:
                                key = ("gather", u, HEADS - 1, T - 1)
                                act.wait_ge(freed(key), readout(it, key))
                            act.activation(Z[u][:, t, :], G[u][:, t, :], ACT.Exp).then_inc(S["elu_exp"], 1)
                    elif name == "turn1":
                        for c in range(T):
                            read(H1T(u, c), lambda b: b[:, :], ("turn1", u, c))
                    elif name == "ffn":
                        for f in range(FC):
                            read(hidden(u, f), lambda b: b[:, :], ("up", u, n, f), ACT.Gelu,
                                 bias=fb1col[:, n, f:f + 1])
                    elif name == "dotproj":
                        for c in range(KC):
                            read(G[u][:, c, :], lambda b: b[:, :], ("hT", u, c), ACT.Identity,
                                 bias=b3col[:, c:c + 1])
                        for c in range(KC):
                            read(G[u][:, KC + c, :], lambda b: b[:, :], ("haT", u, c))
                    elif name == "dotscore":
                        act.wait_ge(S["dotmax"], done(it, "dotmax", u))
                        for t in range(T):
                            ins = act.activation(Z[u][:, t, :], Z[u][:, t, :], ACT.Exp,
                                                 bias=dmax[u][:, 3, t:t + 1], accum_out=dden[u][:, t:t + 1])
                        ins.then_inc(S["dotexp"], 1)
                    elif name == "dotturn":
                        for t in range(T):
                            read(G[u][:, t, :], lambda b: b[:, :], ("probT", u, t))
                    elif name == "dotout":
                        for t in range(T):
                            key = ("dotout", u, t)
                            act.wait_ge(freed(key), readout(it, key))
                            act.activation(Z[u][:, t, D:2 * D], Z[u][:, t, 0:D],
                                           ACT.Exp).then_inc(S["out_exp"], 1)

        @block.tensor
        def _(pe):
            pe.wait_ge(s_const, 4)
            pe.wait_ge(s_w, 16 * len(loads))
            pe.wait_ge(s_fold, 1)
            with pe.Fori(0, TURNS) as it:
                seen = [-1] * BANKS

                def begin(key):
                    b, use = group_at[key] % BANKS, group_at[key] // BANKS
                    if use > seen[b]:
                        seen[b] = use
                        pe.wait_ge(freed(key), readout(it, key) - 1)
                    return bank(key)

                def after(key):
                    b, use = group_at[key] % BANKS, group_at[key] // BANKS
                    if use + 1 > seen[b]:
                        seen[b] = use + 1
                        pe.wait_ge(freed(key), readout(it, key))

                def spread(dst, col):
                    for t in range(T):
                        ins = pe.matmul(dst[:, t * P:(t + 1) * P], col[:, t:t + 1].broadcast_to([P, P]),
                                        ident[:, :], start=True, stop=True)
                    return ins

                def transpose4(key, src):
                    b = begin(key)
                    for t in range(T):
                        ins = pe.transpose(b[:, t * P:(t + 1) * P], src(t), ident[:, :])
                    ins.then_inc(s_mm, 1)

                def product_of(key, width, lhs, rhs, chunks):
                    b = begin(key)
                    for k in range(chunks):
                        ins = pe.matmul(b[:, 0:width], lhs(k), rhs(k), start=(k == 0), stop=(k == chunks - 1))
                    ins.then_inc(s_mm, 1)

                for name, u, n in STEPS:
                    if name == "mask":
                        pe.wait_ge(S["edges"], done(it, "edges", u))
                        for c in range(T):
                            b = begin(("maskT", u, c))[:, :].bitcast(BF16)
                            for t in range(T):
                                ins = pe.transpose(b[:, t * P:(t + 1) * P], M3[u][:, t, c * P:(c + 1) * P],
                                                   identb[:, :])
                            ins.then_inc(s_mm, 1)
                    elif name == "turn":
                        if n in (0, 4):
                            pe.wait_ge(S["normed"], done(it, "normed", (u, 0 if n == 0 else 3)))
                        else:
                            pe.wait_ge(S["layered"], done(it, "layered", (u, 2 * (n - 1))))
                        for c in range(KC):
                            transpose4(("turn", u, n, c), lambda t: HX[u][:, t, c * P:(c + 1) * P])
                    elif name == "proj1":
                        for c in range(KC):
                            after(("turn", u, 0, c))
                        b = begin(("cols1", u))
                        for t in range(T):
                            for k in range(KC):
                                ins = pe.matmul(b[:, t * 2 * HEADS:(t + 1) * 2 * HEADS],
                                                HT[u][:, k, t * P:(t + 1) * P], wa1[:, k, :],
                                                start=(k == 0), stop=(k == KC - 1))
                        ins.then_inc(s_mm, 1)
                        for t in range(T):
                            product_of(("values1", u, t), D1, lambda k: HT[u][:, k, t * P:(t + 1) * P],
                                       lambda k: W1[:, k, :], KC)
                    elif name == "proj2":
                        for c in range(T):
                            after(("turn1", u, c))
                        b = begin(("cols2", u))
                        for t in range(T):
                            for k in range(T):
                                ins = pe.matmul(b[:, t * 2:(t + 1) * 2], H1T(u, k)[:, t * P:(t + 1) * P],
                                                wa2[:, k, :], start=(k == 0), stop=(k == T - 1))
                        ins.then_inc(s_mm, 1)
                        for t in range(T):
                            product_of(("values2", u, t), D, lambda k: H1T(u, k)[:, t * P:(t + 1) * P],
                                       lambda k: W2[:, k, :], T)
                    elif name == "max":
                        if n < HEADS:
                            after(("cols1", u))
                        elif n == HEADS:
                            after(("cols2", u))
                        else:
                            pe.wait_ge(S["cols"], done(it, "cols", (u, n - ATT_L1)))
                        spread(begin(("arow", u, n)), a_cols(u, n)).then_inc(s_mm, 1)
                    elif name == "weights":
                        pe.wait_ge(S["shift"], done(it, "shift", (u, n)))
                        spread(row_lo[u], cols[u][:, n % 2, 4, :]).then_inc(S["rows"], 1)
                        spread(row_hi[u], cols[u][:, n % 2, 3, :]).then_inc(S["rows"], 1)
                    elif name == "gather":
                        pe.wait_ge(S["exp"], done(it, "exp", (u, n, T - 1)))
                        if n < HEADS:
                            for t in range(T):
                                after(("values1", u, t))
                        if n == HEADS:
                            for t in range(T):
                                after(("values2", u, t))
                        width = (HF if n < HEADS else D) + 1
                        for t in range(T):
                            product_of(("gather", u, n, t), width, lambda s: Z[u][:, s, t * P:(t + 1) * P],
                                       lambda s: values(u, n, s), T)
                    elif name == "turn1":
                        pe.wait_ge(S["elu"], done(it, "elu", (u, T - 1)))
                        for c in range(T):
                            transpose4(("turn1", u, c), lambda t: G[u][:, t, c * P:(c + 1) * P])
                    elif name == "ffn":
                        for c in range(KC):
                            after(("turn", u, n + 1, c))
                        for f in range(FC):
                            product_of(("up", u, n, f), N, lambda k: FW1[:, n, k, f * P:(f + 1) * P],
                                       lambda k: HT[u][:, k, :], KC)
                        for f in reversed(range(FC)):
                            after(("up", u, n, f))
                        for t in range(T):
                            product_of(("down", u, n, t), D, lambda k: hidden(u, k)[:, t * P:(t + 1) * P],
                                       lambda k: FW2[:, n, k, :], FC)
                    elif name == "dotproj":
                        for c in range(KC):
                            after(("turn", u, 4, c))
                        for c in range(KC):
                            product_of(("hT", u, c), N, lambda k: W3T[:, k, c * P:(c + 1) * P],
                                       lambda k: HT[u][:, k, :], KC)
                        for t in range(T):
                            product_of(("h", u, t), D, lambda k: HT[u][:, k, t * P:(t + 1) * P],
                                       lambda k: W3T[:, k, :], KC)
                        for c in range(KC):
                            after(("hT", u, c))
                        for c in range(KC):
                            product_of(("haT", u, c), N, lambda k: A3[:, k, c * P:(c + 1) * P],
                                       lambda k: G[u][:, k, :], KC)
                    elif name == "dotscore":
                        for c in range(KC):
                            after(("haT", u, c))
                        for t in range(T):
                            product_of(("dots", u, t), N, lambda k: G[u][:, KC + k, t * P:(t + 1) * P],
                                       lambda k: G[u][:, k, :], KC)
                    elif name == "dotturn":
                        pe.wait_ge(S["dotexp"], done(it, "dotexp", u))
                        for c in range(T):
                            transpose4(("probT", u, c), lambda t: Z[u][:, t, c * P:(c + 1) * P])
                    elif name == "dotout":
                        for t in range(T):
                            after(("probT", u, t))
                            after(("h", u, t))
                        for t in range(T):
                            product_of(("dotout", u, t), D, lambda k: G[u][:, k, t * P:(t + 1) * P],
                                       lambda k: HX[u][:, k, 0:D], T)

        @block.vector
        def _(dve):
            dve.wait_ge(s_w, 16 * len(loads))
            for k in range(KC):
                for c in range(2 * HEADS):
                    h = c % HEADS
                    dve.tensor_tensor_reduce(junk[:, 0, 0:HF], W1[:, k, h * HF:(h + 1) * HF],
                                             G[0][:, c // HEADS, h * HF:(h + 1) * HF], 1.0, 0.0, ALU.mult,
                                             ALU.add, wa1[:, k, c:c + 1]).then_inc(s_dve, 1)
                    dve.wait_ge(s_dve, k * 2 * HEADS + c + 1)
            PRE = KC * 2 * HEADS + 2 * T
            for k in range(T):
                for c in range(2):
                    dve.tensor_tensor_reduce(junk[:, 0, 0:D], W2[:, k, :], G[0][:, 2, c * D:(c + 1) * D], 1.0, 0.0,
                                             ALU.mult, ALU.add, wa2[:, k, c:c + 1]).then_inc(s_dve, 1)
                    dve.wait_ge(s_dve, KC * 2 * HEADS + k * 2 + c + 1)
            dve.memset(gate[:, :], 0.0).then_inc(s_fold, 1)
            dve.wait_ge(s_fold, 1)
            links = [0]
            with dve.Fori(0, TURNS) as it:
                LINKS = UNITS * DVE_LINKS

                def link(ins):
                    links[0] += 1
                    ins.then_inc(s_dve, 1)
                    dve.wait_ge(s_dve, it * LINKS + PRE + links[0])

                def take(ins):
                    links[0] += 1
                    ins.then_inc(s_dve, 1)
                    return it * LINKS + PRE + links[0]

                gates = [0]

                def pass_gate():
                    g = gates[0] % gate.shape[1]
                    gates[0] += 1
                    dve.memset(gate[:, g:g + 1], 0.0)

                def moments(src, key):
                    for t in range(T):
                        ins = dve.bn_stats(stats[u][:, t, :], src(t))
                    link(ins)
                    pass_gate()
                    for t in range(T):
                        ins = dve.bn_aggr(mv[u][:, t, :], stats[u][:, t, :])
                    ins.then_inc(S["moments"], 1)

                for name, u, n in STEPS:
                    if name == "mask":
                        dve.wait_ge(s_adj, it * 16 * UNITS + 16 * (u + 1))
                        link(dve.tensor_scalar(M3[u][:, :, :], edges[:, :, :], 0.0, -BIG, ALU.is_le, ALU.mult))
                        dve.tensor_copy(MN[u][:, :, :], M3[u][:, :, :]).then_inc(S["edges"], 1)
                    elif name == "norm":
                        if n == 0:
                            dve.wait_ge(s_x[u], it * 16 + 16)
                        elif n == 2:
                            dve.wait_ge(S["summed"], done(it, "summed", u))
                        else:
                            key = ("gather", u, HEADS if n == 1 else ATT_L2, T - 1)
                            dve.wait_ge(freed(key), readout(it, key))
                        moments(lambda t: X[u][:, t, :], (u, "n", n))
                    elif name == "affine":
                        l = n // 2
                        key = ("gather", u, ATT_L1 + l, T - 1) if n % 2 == 0 else ("down", u, l, T - 1)
                        dve.wait_ge(freed(key), readout(it, key))
                        src = (lambda t: R1(u, t)) if n % 2 == 0 else (lambda t: Z[u][:, t, 0:D])
                        moments(src, (u, "a", n))
                        dve.wait_ge(S["rstd"], done(it, "rstd", (u, "a", n)))
                        for t in range(T):
                            at = dve.scalar_tensor_tensor(out=src(t), in0=src(t), scalar=mv[u][:, t, 0:1],
                                                          in1=g_row[:, n, :], op0=ALU.subtract, op1=ALU.mult)
                            if t == T - 1:
                                link(at)
                        for t in range(T):
                            ins = dve.scalar_tensor_tensor(out=HX[u][:, t, 0:D], in0=src(t),
                                                           scalar=norm_c[u][:, 1, t:t + 1],
                                                           in1=be_row[:, n, :], op0=ALU.mult, op1=ALU.add)
                        ins.then_inc(S["layered"], 1)
                    elif name in ("proj1", "proj2"):
                        key, dst = (("cols1", u), ab1[u]) if name == "proj1" else (("cols2", u), ab2[u])
                        w = dst.shape[2]
                        dve.wait_ge(s_mm, product(it, key))
                        dve.tensor_copy(dst[:, :, :], bank(key)[:, 0:T * w].rearrange("p (t c) -> p t c", c=w)
                                        ).then_inc(freed(key), 1)
                    elif name == "score":
                        if n < LAYERS and n > 0:
                            dve.wait_ge(S["layered"], done(it, "layered", (u, 2 * n - 1)))
                        else:
                            dve.wait_ge(S["normed"], done(it, "normed", (u, 1 if n == 0 else 2)))
                        pass_gate()
                        for t in range(T):
                            for c in range(2):
                                ins = dve.tensor_tensor_reduce(junk[:, t, c * D:(c + 1) * D], HX[u][:, t, 0:D],
                                                               s_row[:, n, c, :], 1.0, 0.0, ALU.mult, ALU.add,
                                                               ab2[u][:, t, c:c + 1])
                        link(ins)
                        dve.tensor_scalar(ab2[u][:, :, 1], ab2[u][:, :, 1], s_bias[:, n:n + 1], None,
                                          ALU.add).then_inc(S["cols"], 1)
                    elif name == "max":
                        key = ("arow", u, n)
                        c = cols[u][:, n % 2]
                        if n in (0, ATT_L1, ATT_L2, HEADS):
                            dve.wait_ge(S["masks"], done(it, "masks", u))
                        dve.wait_ge(s_mm, product(it, key))
                        for t in range(T):
                            if t == 0:
                                pass_gate()
                            ins = dve.tensor_tensor_reduce(junk[:, t, :], bank(key)[:, :], masks(u, n)[1][:, t, :], 1.0,
                                                           -3e38, ALU.add, ALU.max, c[:, 0, t:t + 1])
                        ins.then_inc(freed(key), 1)
                        dve.wait_ge(freed(key), readout(it, key))
                        a, b = a_cols(u, n), b_cols(u, n)
                        link(dve.tensor_tensor(c[:, 1, :], c[:, 0, :], b, ALU.add))
                        link(dve.scalar_tensor_tensor(out=c[:, 2, :], in0=c[:, 1, :], scalar=SLOPE, in1=c[:, 1, :],
                                                      op0=ALU.mult, op1=ALU.max))
                        dve.tensor_tensor(c[:, 3, :], b, c[:, 2, :], ALU.subtract)
                        dve.tensor_scalar(a_low[u][:, n % 2, :], a, SLOPE, None, ALU.mult)
                        dve.scalar_tensor_tensor(out=c[:, 4, :], in0=b, scalar=SLOPE, in1=c[:, 2, :],
                                                 op0=ALU.mult, op1=ALU.subtract).then_inc(S["shift"], 1)
                    elif name == "weights":
                        dve.wait_ge(S["rows"], done(it, "rows", (u, n, 1)))
                        for t in range(T):
                            dve.wait_ge(S["low"], done(it, "low", (u, n, t)))
                            dve.scalar_tensor_tensor(out=Z[u][:, t, :], in0=row_hi[u][:, :],
                                                     scalar=a_cols(u, n)[:, t:t + 1], in1=LOW[u][:, t % 2, :],
                                                     op0=ALU.add, op1=ALU.max).then_inc(S["high"], 1)
                    elif name == "gather":
                        width = HF if n < HEADS else D
                        if n == HEADS:
                            dve.wait_ge(S["xbias"], done(it, "xbias", u))
                        at = [None] * T

                        def scale(t):
                            key = ("gather", u, n, t)
                            if n < HEADS:
                                dst, add = G[u][:, t, n * HF:(n + 1) * HF], b1row[:, n * HF:(n + 1) * HF]
                            elif n in (HEADS, ATT_L2):
                                dst = add = X[u][:, t, :]
                            else:
                                dst, add = R1(u, t), HX[u][:, t, 0:D]
                            dve.wait_ge(s_dve, at[t])
                            dve.scalar_tensor_tensor(out=dst, in0=bank(key)[:, 0:width], scalar=rden[u][:, t:t + 1],
                                                     in1=add, op0=ALU.mult, op1=ALU.add).then_inc(freed(key), 1)

                        for t in range(T):
                            key = ("gather", u, n, t)
                            dve.wait_ge(s_mm, product(it, key))
                            at[t] = take(dve.reciprocal(rden[u][:, t:t + 1], bank(key)[:, width:width + 1]))
                            if t:
                                scale(t - 1)
                        scale(T - 1)
                    elif name == "elu":
                        for t in range(T):
                            dve.wait_ge(S["elu_exp"], done(it, "elu_exp", (u, t)))
                            link(dve.tensor_scalar(Z[u][:, t, :], Z[u][:, t, :], 1.0, -1.0, ALU.min, ALU.add))
                            dve.scalar_tensor_tensor(out=G[u][:, t, :], in0=G[u][:, t, :], scalar=0.0,
                                                     in1=Z[u][:, t, :], op0=ALU.max, op1=ALU.add
                                                     ).then_inc(S["elu"], 1)
                    elif name == "ffn":
                        dve.wait_ge(S["hbias"], done(it, "hbias", (u, n)))
                        for t in range(T):
                            key = ("down", u, n, t)
                            dve.wait_ge(s_mm, product(it, key))
                            dve.tensor_tensor(Z[u][:, t, 0:D], bank(key)[:, 0:D], HX[u][:, t, 0:D],
                                              ALU.add).then_inc(freed(key), 1)
                    elif name == "dotproj":
                        for t in range(T):
                            key = ("h", u, t)
                            dve.wait_ge(s_mm, product(it, key))
                            dve.tensor_tensor(HX[u][:, t, 0:D], bank(key)[:, 0:D], b3row[:, :],
                                              ALU.add).then_inc(freed(key), 1)
                    elif name == "dotscore":
                        c = dmax[u]
                        for t in range(T):
                            key = ("dots", u, t)
                            dve.wait_ge(s_mm, product(it, key))
                            pass_gate()
                            dve.tensor_tensor_reduce(Z[u][:, t, :], bank(key)[:, :], M3[u][:, t, :], 1.0, -3e38,
                                                     ALU.add, ALU.max, c[:, 0, t:t + 1]).then_inc(freed(key), 1)
                            dve.wait_ge(freed(key), readout(it, key))
                        link(dve.tensor_scalar(c[:, 1, :], c[:, 0, :], 1e9, 0.0, ALU.mult, ALU.min))
                        link(dve.tensor_tensor(c[:, 2, :], c[:, 1, :], c[:, 1, :], ALU.subtract))
                        dve.scalar_tensor_tensor(out=c[:, 3, :], in0=c[:, 0, :], scalar=-1.0, in1=c[:, 2, :],
                                                 op0=ALU.mult, op1=ALU.add).then_inc(S["dotmax"], 1)
                    elif name == "dotturn":
                        dve.wait_ge(S["dotexp"], done(it, "dotexp", u))
                        link(dve.reciprocal(rden[u][:, :], dden[u][:, :]))
                    elif name == "dotout":
                        for t in range(T):
                            key = ("dotout", u, t)
                            dve.wait_ge(s_mm, product(it, key))
                            dve.tensor_scalar(Z[u][:, t, 0:D], bank(key)[:, 0:D], rden[u][:, t:t + 1], None,
                                              ALU.mult).then_inc(freed(key), 1)
                        for t in range(T):
                            dve.wait_ge(S["out_exp"], done(it, "out_exp", (u, t)))
                            e, y = Z[u][:, t, D:2 * D], Z[u][:, t, 0:D]
                            link(dve.tensor_scalar(e, e, 1.0, -1.0, ALU.min, ALU.add))
                            link(dve.scalar_tensor_tensor(out=y, in0=y, scalar=0.0, in1=e, op0=ALU.max,
                                                          op1=ALU.add))
                            ins = dve.tensor_tensor(X[u][:, t, :], X[u][:, t, :], y, ALU.add)
                        ins.then_inc(S["out"], 1)
                assert links[0] == LINKS, links[0]


DVE_LINKS = 1 + (4 + 6) + 6 + 4 + 9 * 2 + 9 * 4 + 4 + 2 + 1 + 4 * 2

_INS = ["x", "adj", "L0_gnn_W1", "L0_gnn_att_src1", "L0_gnn_att_dst1", "L0_gnn_b1", "L0_gnn_W2",
        "L0_gnn_att_src2", "L0_gnn_att_dst2", "L0_gnn_b2", "L1_gnn_attn_w", "L1_gnn_attn_b", "L1_gnn_W1",
        "L1_gnn_b1", "L1_gnn_W2", "L1_gnn_b2", "L1_gnn_g1", "L1_gnn_beta1", "L1_gnn_g2", "L1_gnn_beta2",
        "L2_gnn_attn_w_src", "L2_gnn_attn_w_dst", "L2_gnn_attn_b", "L3_gnn_W", "L3_gnn_b", "L3_gnn_attn"]


def kernel(**inputs):
    import numpy as np
    import concourse.bacc as bacc
    from concourse.bass_utils import run_bass_kernel_spmd as run

    nc = bacc.Bacc("TRN2", target_bir_lowering=False, num_devices=1)
    arrays, args = {}, []
    for name in _INS + ["b3_by_part"]:
        a = np.asarray(inputs["L3_gnn_b" if name == "b3_by_part" else name])
        if name == "L1_gnn_b1":
            a = a.reshape(a.shape[0], -1, P).transpose(2, 0, 1)
        if name == "b3_by_part":
            a = a.reshape(-1, P).T
        if name == "L3_gnn_W":
            a = a.T
        a = np.ascontiguousarray(a)
        arrays[f"in_{name}"] = a
        args.append(nc.dram_tensor(f"in_{name}", a.shape, mybir.dt.from_np(a.dtype), kind="ExternalInput").ap())
    out = nc.dram_tensor("out", inputs["x"].shape, F32, kind="ExternalOutput").ap()
    gnn_kernel(nc, *args, out)
    r = run(nc, [arrays], core_ids=[0])
    return r.results[0]["out"]
```

```python
from contextlib import ExitStack

import concourse.bass as bass
from concourse import mybir

ALU = mybir.AluOpType
ACT = mybir.ActivationFunctionType
F32 = mybir.dt.float32
BF16 = mybir.dt.bfloat16
I32 = mybir.dt.int32

P = 128
UNITS = 2
BANKS = 4
BIG = 1e30
SLOPE = 0.2
EPS = 1e-5
HEADS = 4
ATT_L1, ATT_L2 = HEADS + 1, HEADS + 4


def steps_of():
    s = [("load", 0), ("mask", 0), ("norm", 0), ("turn", 0), ("proj1", 0), ("max", 0)]
    for h in range(HEADS):
        s.append(("weights", h))
        if h + 1 < HEADS:
            s.append(("max", h + 1))
        s.append(("gather", h))
    s += [("elu", 0), ("turn1", 0), ("proj2", 0), ("max", HEADS), ("weights", HEADS), ("gather", HEADS)]
    s.append(("norm", 1))
    for l in range(3):
        a = ATT_L1 + l
        s += [("score", l), ("max", a), ("weights", a), ("gather", a), ("affine", 2 * l), ("turn", 1 + l)]
        s += [("up", (l, i)) for i in range(FFN_PARTS)]
        s += [("down", (l, i)) for i in range(FFN_PARTS)]
        s.append(("affine", 2 * l + 1))
    s += [("resid", 0), ("norm", 2), ("score", 3), ("max", ATT_L2), ("weights", ATT_L2), ("gather", ATT_L2)]
    s += [("norm", 3), ("turn", 4), ("dotproj", 0), ("dotscore", 0), ("dotturn", 0), ("dotout", 0), ("store", 0)]
    return s


BEHIND = 3
WHOSE_STEP = ("001011010001100100110001010110101011001101101010010100100110"
              "010100110001111001011001111000010100110001011101011001110010"
              "01010011000111100011010111011001101010101110")


def interleave():
    steps = steps_of()
    at = [0, len(steps) - BEHIND]
    turn = []
    for u in map(int, WHOSE_STEP):
        name, n = steps[at[u] % len(steps)]
        turn.append((name, u, n, -1 if u and at[u] < len(steps) else 0))
        at[u] += 1
    assert at == [len(steps), 2 * len(steps) - BEHIND]
    return turn


FFN_PARTS = 4
TURN = interleave()
FIRST_TURN = [s for s in TURN if s[3] == 0]
LAST_TURN = [s for s in TURN if s[3] < 0]


def plan(T, KC, FC):
    groups, marks = [], {}

    def mark(name, *keys):
        marks.setdefault(name, []).extend(keys)

    for name, n in steps_of():
        if name == "mask":
            mark("edges", 0)
            mark("masks", 0)
            groups += [("maskT", c) for c in range(T)]
        elif name == "norm":
            mark("moments", ("n", n))
            mark("rstd", ("n", n))
            mark("normed", n)
            if n == 0:
                mark("xbias", 0)
        elif name == "affine":
            mark("moments", ("a", n))
            mark("rstd", ("a", n))
            mark("layered", n)
        elif name == "turn":
            groups += [("turn", n, c) for c in range(KC)]
            if 1 <= n <= 3:
                mark("hbias", n - 1)
        elif name == "proj1":
            groups += [("cols1",)] + [("values1", t) for t in range(T)]
            mark("ones1", 0)
        elif name == "proj2":
            groups += [("cols2",)] + [("values2", t) for t in range(T)]
        elif name == "score":
            mark("cols", n)
        elif name == "max":
            groups.append(("arow", n))
            mark("shift", n)
        elif name == "weights":
            groups += [("lo", n), ("hi", n)]
            for t in range(T):
                if t < T - 1:
                    mark("low", (n, t))
                    mark("high", (n, t))
                mark("masked", (n, t))
                mark("exp", (n, t))
        elif name == "gather":
            groups += [("gather", n, t) for t in range(T)]
        elif name == "elu":
            mark("elu_exp", *range(T))
            mark("elu", *range(T))
        elif name == "turn1":
            groups += [("turn1", c) for c in range(T)]
        elif name == "up":
            each = FC // FFN_PARTS
            groups += [("up", n[0], f) for f in range(n[1] * each, (n[1] + 1) * each)]
        elif name == "down":
            groups.append(("down", n[0], n[1]))
        elif name == "resid":
            mark("summed", 0)
        elif name == "dotproj":
            groups += [("hT", c) for c in range(KC)] + [("h", t) for t in range(T)]
            groups += [("haT", c) for c in range(KC)]
        elif name == "dotscore":
            groups += [("dots", t) for t in range(T)]
            mark("dotmax", 0)
            mark("dotexp", 0)
        elif name == "dotturn":
            groups += [("probT", t) for t in range(T)]
        elif name == "dotout":
            groups += [("dotout", t) for t in range(T)]
            mark("out_exp", *range(T))
            mark("out", 0)
    return groups, marks


def gnn_kernel(nc, x, adj, w1, as1, ad1, b1, w2, as2, ad2, b2, aw, ab, fw1, fb1, fw2, fb2, g1, be1, g2, be2,
               sw, dw, sb2, w3t, b3, attn3, b3_by_part, out):
    B, N, D = x.shape
    T = N // P
    KC = D // P
    HF = w1.shape[1] // HEADS
    D1 = HEADS * HF
    LAYERS, _, FF = fw1.shape
    FC = FF // P
    TURNS = B // UNITS
    assert HF == P and D1 == N and T == HEADS and FC == 2 * T

    groups, marks = plan(T, KC, FC)
    group_at = {g: i for i, g in enumerate(groups)}
    mark_at = {name: {k: i for i, k in enumerate(keys)} for name, keys in marks.items()}
    uses_of_bank = [len(range(b, len(groups), BANKS)) for b in range(BANKS)]

    with ExitStack() as ctx:
        def sb(name, shape, dt=F32):
            return ctx.enter_context(nc.sbuf_tensor(name, shape, dt))

        def sem(name):
            return ctx.enter_context(nc.semaphore(name))

        W1 = sb("W1", [P, KC, D1])
        W2 = sb("W2", [P, T, D])
        FW1 = sb("FW1", [P, LAYERS, KC, FF])
        FW2 = sb("FW2", [P, LAYERS, FC, D])
        W3T = sb("W3T", [P, KC, D])
        A3 = sb("A3", [P, KC, D])
        b1row = sb("b1row", [P, D1])
        b2row = sb("b2row", [P, D])
        g_row = sb("g_row", [P, 2 * LAYERS, D])
        be_row = sb("be_row", [P, 2 * LAYERS, D])
        fb2row = sb("fb2row", [P, LAYERS, D])
        s_row = sb("s_row", [P, LAYERS + 1, 2, D])
        s_bias = sb("s_bias", [P, LAYERS + 1])
        b3row = sb("b3row", [P, D])
        fb1col = sb("fb1col", [P, LAYERS, FC])
        b3col = sb("b3col", [P, KC])
        wa1 = sb("wa1", [P, KC, 2 * HEADS])
        wa2 = sb("wa2", [P, T, 2])
        ident = sb("ident", [P, P])
        identb = sb("identb", [P, P], BF16)
        offdiag = sb("offdiag", [P, P], BF16)
        c_eps = sb("c_eps", [P, T])
        c_neg1 = sb("c_neg1", [P, T])
        c_half = sb("c_half", [P, T])
        edges = sb("edges", [P, T, N], I32)

        def per_unit(name, shape, dt=F32):
            return [sb(f"{name}{u}", shape, dt) for u in range(UNITS)]

        X = per_unit("X", [P, T, D])
        HX = per_unit("HX", [P, T, D + 1])
        HT = per_unit("HT", [P, KC, N])
        M3 = per_unit("M3", [P, T, N], BF16)
        MN = per_unit("MN", [P, T, N], BF16)
        MT = per_unit("MT", [P, T, N], BF16)
        LOW = per_unit("LOW", [P, 2, N])
        Z = per_unit("Z", [P, T, N])
        G = per_unit("G", [P, T, N])
        V1 = per_unit("V1", [P, T, HEADS * (HF + 1)])
        ab1 = per_unit("ab1", [P, T, 2 * HEADS])
        ab2 = per_unit("ab2", [P, T, 2])
        cols = per_unit("cols", [P, 2, 5, T])
        a_low = per_unit("a_low", [P, 2, T])
        stats = per_unit("stats", [P, T, 6])
        mv = per_unit("mv", [P, T, 2])
        norm_c = per_unit("norm_c", [P, 4, T])
        rden = per_unit("rden", [P, T])
        dmax = per_unit("dmax", [P, 4, T])
        dden = per_unit("dden", [P, T])

        gate = per_unit("gate", [P, 64])

        ring = [[ctx.enter_context(nc.psum_tensor(f"ring{u}{b}", [P, N], F32)) for b in range(BANKS)]
                for u in range(UNITS)]

        s_w = sem("weights_loaded")
        s_const = sem("constants_set")
        s_fold = sem("score_weights_folded")
        s_x = [sem(f"x_loaded{u}") for u in range(UNITS)]
        s_adj = [sem(f"adj_loaded{u}") for u in range(UNITS)]
        s_store = [sem(f"stored{u}") for u in range(UNITS)]
        s_mm = [sem(f"product_done{u}") for u in range(UNITS)]
        s_free = [[sem(f"bank_read{u}{b}") for b in range(BANKS)] for u in range(UNITS)]
        s_pre = sem("folding_step")
        s_dve = [sem(f"vector_step{u}") for u in range(UNITS)]
        s_pool = [sem(f"pool_step{u}") for u in range(UNITS)]
        S = {name: [sem(f"{name}_done{u}") for u in range(UNITS)] for name in marks}

        SEED = 1

        def bank(u, key):
            return ring[u][group_at[key] % BANKS]

        def freed(u, key):
            return s_free[u][group_at[key] % BANKS]

        def product(g, key):
            return g * len(groups) + group_at[key] + 1

        def readout(g, key):
            i = group_at[key]
            return SEED + g * uses_of_bank[i % BANKS] + i // BANKS + 1

        def done(g, name, key):
            return g * len(marks[name]) + mark_at[name][key] + 1

        def V1h(u, t, h):
            return V1[u][:, t, h * (HF + 1):(h + 1) * (HF + 1)]

        def H1T(u, c):
            return V1[u][:, :, :].rearrange("p t n -> p (t n)")[:, c * N:(c + 1) * N]

        def hidden(u, f):
            return G[u][:, f, :] if f < T else H1T(u, f - T)

        def R1(u, t):
            return G[u][:, :, :].rearrange("p t n -> p (t n)")[:, t * D:(t + 1) * D]

        def junk(u, t):
            return LOW[u][:, t // 2, :].bitcast(BF16)[:, (t % 2) * N:(t % 2 + 1) * N]

        def a_cols(u, n):
            return ab1[u][:, :, n] if n < HEADS else ab2[u][:, :, 0]

        def b_cols(u, n):
            return ab1[u][:, :, HEADS + n] if n < HEADS else ab2[u][:, :, 1]

        def masks(u, n):
            return (MN[u], MT[u]) if n <= HEADS else (MT[u], MN[u])

        def values(u, n, t):
            return V1h(u, t, n) if n < HEADS else HX[u][:, t, :]

        nodes = "b (t p) d -> b p t d"
        x_v, adj_v, out_v = (a.rearrange(nodes, p=P) for a in (x, adj, out))

        nc.disable_value_cache = True
        block = ctx.enter_context(nc.Block())
        loads = [
            (W1[:, :, :], w1.rearrange("(k p) n -> p k n", p=P)),
            (W2[:, :, :], w2.rearrange("(k p) n -> p k n", p=P)),
            (W3T[:, :, :], w3t.rearrange("(k p) n -> p k n", p=P)),
            (A3[:, :, :], attn3.rearrange("(k p) n -> p k n", p=P)),
            (b1row[:, :], b1.partition_broadcast(P)),
            (b2row[:, :], b2.partition_broadcast(P)),
            (b3row[:, :], b3.partition_broadcast(P)),
            (fb1col[:, :, :], fb1),
            (b3col[:, :], b3_by_part),
            (fb2row[:, :, :], fb2.partition_broadcast(P)),
            (s_row[:, LAYERS, 0, :], dw.partition_broadcast(P)),
            (s_row[:, LAYERS, 1, :], sw.partition_broadcast(P)),
            (s_bias[:, 0:LAYERS], ab.partition_broadcast(P)),
            (s_bias[:, LAYERS:LAYERS + 1], sb2.partition_broadcast(P)),
            (G[0][:, 0, :], as1.rearrange("h f -> (h f)").partition_broadcast(P)),
            (G[0][:, 1, :], ad1.rearrange("h f -> (h f)").partition_broadcast(P)),
            (G[0][:, 2, 0:D], as2.rearrange("h f -> (h f)").partition_broadcast(P)),
            (G[0][:, 2, D:2 * D], ad2.rearrange("h f -> (h f)").partition_broadcast(P)),
        ]
        for l in range(LAYERS):
            loads += [
                (FW1[:, l, :, :], fw1[l].rearrange("(k p) n -> p k n", p=P)),
                (FW2[:, l, :, :], fw2[l].rearrange("(k p) n -> p k n", p=P)),
                (g_row[:, 2 * l, :], g1[l].partition_broadcast(P)),
                (g_row[:, 2 * l + 1, :], g2[l].partition_broadcast(P)),
                (be_row[:, 2 * l, :], be1[l].partition_broadcast(P)),
                (be_row[:, 2 * l + 1, :], be2[l].partition_broadcast(P)),
                (s_row[:, l, 1, :], aw[l, 0:D].partition_broadcast(P)),
                (s_row[:, l, 0, :], aw[l, D:2 * D].partition_broadcast(P)),
            ]

        @block.sync
        def _(sp):
            for u in range(UNITS):
                for free in s_free[u]:
                    sp.sem_inc(free, SEED)
                sp.sem_inc(s_store[u], 16 * SEED)
            for dst, src in loads:
                sp.dma_start(dst, src).then_inc(s_w, 16)

            def run(steps, it):
                for name, u, n, back in steps:
                    g = it + back
                    if name == "load":
                        sp.wait_ge(s_store[u], 16 * SEED + g * 16)
                        sp.dma_start(X[u][:, :, :], x_v[g * UNITS + u]).then_inc(s_x[u], 16)
                        if u == 1 or steps is TURN:
                            sp.wait_ge(S["edges"][1 - u], g + u)
                        sp.dma_start(edges[:, :, :], adj_v[g * UNITS + u]).then_inc(s_adj[u], 16)
                    elif name == "store":
                        sp.wait_ge(S["out"][u], done(g, "out", 0))
                        sp.dma_start(out_v[g * UNITS + u], X[u][:, :, :]).then_inc(s_store[u], 16)

            run(FIRST_TURN, 0)
            with sp.Fori(1, TURNS) as it:
                run(TURN, it)
            run(LAST_TURN, TURNS)
            for u in range(UNITS):
                sp.wait_ge(s_store[u], 16 * SEED + 16 * TURNS)

        @block.gpsimd
        def _(pool):
            pool.memset(ident[:, :], 0.0)
            pool.memset(identb[:, :], 0.0)
            pool.memset(offdiag[:, :], 1.0)
            pool.memset(c_eps[:, :], EPS)
            pool.memset(c_neg1[:, :], -1.0)
            for u in range(UNITS):
                pool.memset(HX[u][:, :, D:D + 1], 1.0)
            pool.memset(c_half[:, :], -0.5).then_inc(s_const, 1)
            pool.wait_ge(s_const, 1)
            for m, v in ((ident, 1.0), (identb, 1.0), (offdiag, 0.0)):
                pool.affine_select(out=m[:, :], in_=m[:, :], compare_op=ALU.not_equal, fill=v, base=0,
                                   pattern=[[-1, P]], channel_multiplier=1).then_inc(s_const, 1)
            pool.wait_ge(s_const, 4)
            pool.wait_ge(s_w, 16 * len(loads))
            links = [0] * UNITS

            def run(steps, it):
                def link(ins):
                    links[u] += 1
                    ins.then_inc(s_pool[u], 1)
                    pool.wait_ge(s_pool[u], g * POOL_LINKS + links[u])

                for name, u, n, back in steps:
                    g = it + back
                    if name == "mask":
                        pool.wait_ge(S["edges"][u], done(g, "edges", 0))
                        for t in range(T):
                            d = MN[u][:, t, t * P:(t + 1) * P]
                            pool.tensor_tensor(d, d, offdiag[:, :], ALU.mult)
                        for t in range(T):
                            pool.wait_ge(freed(u, ("maskT", t)), readout(g, ("maskT", t)))
                            d = MT[u][:, t, t * P:(t + 1) * P]
                            ins = pool.tensor_tensor(d, d, offdiag[:, :], ALU.mult)
                        ins.then_inc(S["masks"][u], 1)
                    elif name in ("norm", "affine"):
                        key = (name[0], n)
                        pool.wait_ge(S["moments"][u], done(g, "moments", key))
                        c = norm_c[u]
                        pool.tensor_tensor(c[:, 2, :], mv[u][:, :, 0], c_neg1[:, :], ALU.mult)
                        link(pool.tensor_tensor(c[:, 0, :], mv[u][:, :, 1], c_eps[:, :], ALU.add))
                        link(pool.tensor_tensor(c[:, 1, :], c[:, 0, :], c_half[:, :], ALU.pow))
                        pool.tensor_tensor(c[:, 3, :], c[:, 2, :], c[:, 1, :], ALU.mult).then_inc(S["rstd"][u], 1)
                        if name == "norm" and n == 0:
                            pool.wait_ge(S["normed"][u], done(g, "normed", 0))
                            for t in range(T):
                                ins = pool.tensor_tensor(X[u][:, t, :], X[u][:, t, :], b2row[:, :], ALU.add)
                            ins.then_inc(S["xbias"][u], 1)
                    elif name == "proj1":
                        ones = V1[u][:, :, :].rearrange("p t (h f) -> p t h f", h=HEADS)[:, :, :, HF]
                        pool.memset(ones, 1.0).then_inc(S["ones1"][u], 1)
                    elif name == "turn" and 1 <= n <= LAYERS:
                        pool.wait_ge(s_mm[u], product(g, ("turn", n, KC - 1)))
                        for t in range(T):
                            ins = pool.tensor_tensor(HX[u][:, t, 0:D], HX[u][:, t, 0:D], fb2row[:, n - 1, :],
                                                     ALU.add)
                        ins.then_inc(S["hbias"][u], 1)
                    elif name == "weights":
                        for t in range(T):
                            if t < T - 1:
                                pool.wait_ge(S["high"][u], done(g, "high", (n, t)))
                            else:
                                pool.wait_ge(freed(u, ("hi", n)), readout(g, ("hi", n)))
                            pool.tensor_tensor(Z[u][:, t, :], Z[u][:, t, :], masks(u, n)[0][:, t, :],
                                               ALU.add).then_inc(S["masked"][u], 1)
                    elif name == "resid":
                        pool.wait_ge(S["layered"][u], done(g, "layered", 2 * LAYERS - 1))
                        link(pool.tensor_tensor(X[u][:, 0:T // 2, :], X[u][:, 0:T // 2, :],
                                                HX[u][:, 0:T // 2, 0:D], ALU.add))
                        pool.tensor_tensor(X[u][:, T // 2:T, :], X[u][:, T // 2:T, :],
                                           HX[u][:, T // 2:T, 0:D], ALU.add).then_inc(S["summed"][u], 1)
                    elif name == "store":
                        assert links[u] == POOL_LINKS, links[u]
                        links[u] = 0

            run(FIRST_TURN, 0)
            with pool.Fori(1, TURNS) as it:
                run(TURN, it)
            run(LAST_TURN, TURNS)

        @block.scalar
        def _(act):
            act.wait_ge(s_w, 16 * len(loads))

            def run(steps, it):
                def read(dst, src_of, key, func=ACT.Copy, **kw):
                    act.wait_ge(s_mm[u], product(g, key))
                    act.activation(dst, src_of(bank(u, key)), func, **kw).then_inc(freed(u, key), 1)

                for name, u, n, back in steps:
                    g = it + back
                    if name == "mask":
                        for c in range(T):
                            read(MT[u][:, c, :], lambda b: b[:, :].bitcast(BF16)[:, 0:N], ("maskT", c))
                    elif name == "norm":
                        act.wait_ge(S["rstd"][u], done(g, "rstd", ("n", n)))
                        for t in range(T):
                            ins = act.activation(HX[u][:, t, 0:D], X[u][:, t, :], ACT.Relu,
                                                 bias=norm_c[u][:, 3, t:t + 1], scale=norm_c[u][:, 1, t:t + 1])
                        ins.then_inc(S["normed"][u], 1)
                    elif name == "turn":
                        for c in range(KC):
                            read(HT[u][:, c, :], lambda b: b[:, :], ("turn", n, c))
                    elif name == "proj1":
                        act.wait_ge(S["ones1"][u], done(g, "ones1", 0))
                        for t in range(T):
                            v = V1[u][:, t, :].rearrange("p (h f) -> p h f", h=HEADS)[:, :, 0:HF]
                            read(v, lambda b: b[:, :].rearrange("p (h f) -> p h f", h=HEADS), ("values1", t))
                    elif name == "proj2":
                        for t in range(T):
                            read(HX[u][:, t, 0:D], lambda b: b[:, 0:D], ("values2", t))
                    elif name == "weights":
                        def low(t):
                            if t == 0:
                                act.wait_ge(s_mm[u], product(g, ("lo", n)))
                            if t >= 2:
                                act.wait_ge(S["high"][u], done(g, "high", (n, t - 2)))
                            last = t == T - 1
                            act.activation(LOW[u][:, t % 2, :], bank(u, ("lo", n))[:, :], ACT.Identity,
                                           bias=a_low[u][:, n % 2, t:t + 1]
                                           ).then_inc(freed(u, ("lo", n)) if last else S["low"][u], 1)

                        def exp(t):
                            act.wait_ge(S["masked"][u], done(g, "masked", (n, t)))
                            act.activation(Z[u][:, t, :], Z[u][:, t, :], ACT.Exp).then_inc(S["exp"][u], 1)

                        low(0)
                        low(1)
                        for t in range(2, T):
                            low(t)
                            exp(t - 2)
                        exp(T - 2)
                        exp(T - 1)
                    elif name == "elu":
                        for t in range(T):
                            if t == 0:
                                key = ("gather", HEADS - 1, T - 1)
                                act.wait_ge(freed(u, key), readout(g, key))
                            act.activation(Z[u][:, t, :], G[u][:, t, :], ACT.Exp).then_inc(S["elu_exp"][u], 1)
                    elif name == "turn1":
                        for c in range(T):
                            read(H1T(u, c), lambda b: b[:, :], ("turn1", c))
                    elif name == "up":
                        l, part = n
                        for f in range(part * FC // FFN_PARTS, (part + 1) * FC // FFN_PARTS):
                            read(hidden(u, f), lambda b: b[:, :], ("up", l, f), ACT.Gelu,
                                 bias=fb1col[:, l, f:f + 1])
                    elif name == "dotproj":
                        for c in range(KC):
                            read(G[u][:, c, :], lambda b: b[:, :], ("hT", c), ACT.Identity,
                                 bias=b3col[:, c:c + 1])
                        for c in range(KC):
                            read(G[u][:, KC + c, :], lambda b: b[:, :], ("haT", c))
                    elif name == "dotscore":
                        act.wait_ge(S["dotmax"][u], done(g, "dotmax", 0))
                        for t in range(T):
                            ins = act.activation(Z[u][:, t, :], Z[u][:, t, :], ACT.Exp,
                                                 bias=dmax[u][:, 3, t:t + 1], accum_out=dden[u][:, t:t + 1])
                        ins.then_inc(S["dotexp"][u], 1)
                    elif name == "dotturn":
                        for t in range(T):
                            read(G[u][:, t, :], lambda b: b[:, :], ("probT", t))
                    elif name == "dotout":
                        for t in range(T):
                            key = ("dotout", t)
                            act.wait_ge(freed(u, key), readout(g, key))
                            act.activation(Z[u][:, t, D:2 * D], Z[u][:, t, 0:D],
                                           ACT.Exp).then_inc(S["out_exp"][u], 1)

            run(FIRST_TURN, 0)
            with act.Fori(1, TURNS) as it:
                run(TURN, it)
            run(LAST_TURN, TURNS)

        @block.tensor
        def _(pe):
            pe.wait_ge(s_const, 4)
            pe.wait_ge(s_w, 16 * len(loads))
            pe.wait_ge(s_fold, 1)
            seen = [[-1] * BANKS for _ in range(UNITS)]

            def run(steps, it):
                def begin(key):
                    b, use = group_at[key] % BANKS, group_at[key] // BANKS
                    if use > seen[u][b]:
                        seen[u][b] = use
                        pe.wait_ge(freed(u, key), readout(g, key) - 1)
                    return bank(u, key)

                def after(key):
                    b, use = group_at[key] % BANKS, group_at[key] // BANKS
                    if use + 1 > seen[u][b]:
                        seen[u][b] = use + 1
                        pe.wait_ge(freed(u, key), readout(g, key))

                def spread(dst, col):
                    for t in range(T):
                        ins = pe.matmul(dst[:, t * P:(t + 1) * P], col[:, t:t + 1].broadcast_to([P, P]),
                                        ident[:, :], start=True, stop=True)
                    return ins

                def transpose4(key, src):
                    b = begin(key)
                    for t in range(T):
                        ins = pe.transpose(b[:, t * P:(t + 1) * P], src(t), ident[:, :])
                    ins.then_inc(s_mm[u], 1)

                def product_of(key, width, lhs, rhs, chunks):
                    b = begin(key)
                    for k in range(chunks):
                        ins = pe.matmul(b[:, 0:width], lhs(k), rhs(k), start=(k == 0), stop=(k == chunks - 1))
                    ins.then_inc(s_mm[u], 1)

                for name, u, n, back in steps:
                    g = it + back
                    if name == "mask":
                        pe.wait_ge(S["edges"][u], done(g, "edges", 0))
                        for c in range(T):
                            b = begin(("maskT", c))[:, :].bitcast(BF16)
                            for t in range(T):
                                ins = pe.transpose(b[:, t * P:(t + 1) * P], M3[u][:, t, c * P:(c + 1) * P],
                                                   identb[:, :])
                            ins.then_inc(s_mm[u], 1)
                    elif name == "turn":
                        if n in (0, 4):
                            pe.wait_ge(S["normed"][u], done(g, "normed", 0 if n == 0 else 3))
                        else:
                            pe.wait_ge(S["layered"][u], done(g, "layered", 2 * (n - 1)))
                        for c in range(KC):
                            transpose4(("turn", n, c), lambda t: HX[u][:, t, c * P:(c + 1) * P])
                    elif name == "proj1":
                        for c in range(KC):
                            after(("turn", 0, c))
                        b = begin(("cols1",))
                        for t in range(T):
                            for k in range(KC):
                                ins = pe.matmul(b[:, t * 2 * HEADS:(t + 1) * 2 * HEADS],
                                                HT[u][:, k, t * P:(t + 1) * P], wa1[:, k, :],
                                                start=(k == 0), stop=(k == KC - 1))
                        ins.then_inc(s_mm[u], 1)
                        for t in range(T):
                            product_of(("values1", t), D1, lambda k: HT[u][:, k, t * P:(t + 1) * P],
                                       lambda k: W1[:, k, :], KC)
                    elif name == "proj2":
                        for c in range(T):
                            after(("turn1", c))
                        b = begin(("cols2",))
                        for t in range(T):
                            for k in range(T):
                                ins = pe.matmul(b[:, t * 2:(t + 1) * 2], H1T(u, k)[:, t * P:(t + 1) * P],
                                                wa2[:, k, :], start=(k == 0), stop=(k == T - 1))
                        ins.then_inc(s_mm[u], 1)
                        for t in range(T):
                            product_of(("values2", t), D, lambda k: H1T(u, k)[:, t * P:(t + 1) * P],
                                       lambda k: W2[:, k, :], T)
                    elif name == "max":
                        if n < HEADS:
                            after(("cols1",))
                        elif n == HEADS:
                            after(("cols2",))
                        else:
                            pe.wait_ge(S["cols"][u], done(g, "cols", n - ATT_L1))
                        spread(begin(("arow", n)), a_cols(u, n)).then_inc(s_mm[u], 1)
                    elif name == "weights":
                        pe.wait_ge(S["shift"][u], done(g, "shift", n))
                        spread(begin(("lo", n)), cols[u][:, n % 2, 4, :]).then_inc(s_mm[u], 1)
                        spread(begin(("hi", n)), cols[u][:, n % 2, 3, :]).then_inc(s_mm[u], 1)
                    elif name == "gather":
                        pe.wait_ge(S["exp"][u], done(g, "exp", (n, T - 1)))
                        if n < HEADS:
                            for t in range(T):
                                after(("values1", t))
                        if n == HEADS:
                            for t in range(T):
                                after(("values2", t))
                        width = (HF if n < HEADS else D) + 1
                        for t in range(T):
                            product_of(("gather", n, t), width, lambda s: Z[u][:, s, t * P:(t + 1) * P],
                                       lambda s: values(u, n, s), T)
                    elif name == "turn1":
                        pe.wait_ge(S["elu"][u], done(g, "elu", T - 1))
                        for c in range(T):
                            transpose4(("turn1", c), lambda t: G[u][:, t, c * P:(c + 1) * P])
                    elif name == "up":
                        l, part = n
                        if part == 0:
                            for c in range(KC):
                                after(("turn", l + 1, c))
                        for f in range(part * FC // FFN_PARTS, (part + 1) * FC // FFN_PARTS):
                            product_of(("up", l, f), N, lambda k: FW1[:, l, k, f * P:(f + 1) * P],
                                       lambda k: HT[u][:, k, :], KC)
                    elif name == "down":
                        l, t = n
                        if t == 0:
                            for f in reversed(range(FC)):
                                after(("up", l, f))
                        product_of(("down", l, t), D, lambda k: hidden(u, k)[:, t * P:(t + 1) * P],
                                   lambda k: FW2[:, l, k, :], FC)
                    elif name == "dotproj":
                        for c in range(KC):
                            after(("turn", 4, c))
                        for c in range(KC):
                            product_of(("hT", c), N, lambda k: W3T[:, k, c * P:(c + 1) * P],
                                       lambda k: HT[u][:, k, :], KC)
                        for t in range(T):
                            product_of(("h", t), D, lambda k: HT[u][:, k, t * P:(t + 1) * P],
                                       lambda k: W3T[:, k, :], KC)
                        for c in range(KC):
                            after(("hT", c))
                        for c in range(KC):
                            product_of(("haT", c), N, lambda k: A3[:, k, c * P:(c + 1) * P],
                                       lambda k: G[u][:, k, :], KC)
                    elif name == "dotscore":
                        for c in range(KC):
                            after(("haT", c))
                        for t in range(T):
                            product_of(("dots", t), N, lambda k: G[u][:, KC + k, t * P:(t + 1) * P],
                                       lambda k: G[u][:, k, :], KC)
                    elif name == "dotturn":
                        pe.wait_ge(S["dotexp"][u], done(g, "dotexp", 0))
                        for c in range(T):
                            transpose4(("probT", c), lambda t: Z[u][:, t, c * P:(c + 1) * P])
                    elif name == "dotout":
                        for t in range(T):
                            after(("probT", t))
                            after(("h", t))
                        for t in range(T):
                            product_of(("dotout", t), D, lambda k: G[u][:, k, t * P:(t + 1) * P],
                                       lambda k: HX[u][:, k, 0:D], T)
                        seen[u] = [-1] * BANKS

            run(FIRST_TURN, 0)
            with pe.Fori(1, TURNS) as it:
                run(TURN, it)
            run(LAST_TURN, TURNS)

        @block.vector
        def _(dve):
            dve.wait_ge(s_w, 16 * len(loads))
            for k in range(KC):
                for c in range(2 * HEADS):
                    h = c % HEADS
                    dve.tensor_tensor_reduce(junk(0, 0)[:, 0:HF], W1[:, k, h * HF:(h + 1) * HF],
                                             G[0][:, c // HEADS, h * HF:(h + 1) * HF], 1.0, 0.0, ALU.mult,
                                             ALU.add, wa1[:, k, c:c + 1]).then_inc(s_pre, 1)
                    dve.wait_ge(s_pre, k * 2 * HEADS + c + 1)
            for k in range(T):
                for c in range(2):
                    dve.tensor_tensor_reduce(junk(0, 0)[:, 0:D], W2[:, k, :], G[0][:, 2, c * D:(c + 1) * D], 1.0, 0.0,
                                             ALU.mult, ALU.add, wa2[:, k, c:c + 1]).then_inc(s_pre, 1)
                    dve.wait_ge(s_pre, KC * 2 * HEADS + k * 2 + c + 1)
            dve.memset(gate[0][:, :], 0.0).then_inc(s_fold, 1)
            dve.wait_ge(s_fold, 1)
            links = [0] * UNITS
            gates = [0] * UNITS

            def run(steps, it):
                def take(ins):
                    links[u] += 1
                    ins.then_inc(s_dve[u], 1)
                    return g * DVE_LINKS + links[u]

                def link(ins):
                    dve.wait_ge(s_dve[u], take(ins))

                def pass_gate():
                    dve.memset(gate[u][:, gates[u]:gates[u] + 1], 0.0)
                    gates[u] += 1

                def moments(src, key):
                    for t in range(T):
                        ins = dve.bn_stats(stats[u][:, t, :], src(t))
                    link(ins)
                    pass_gate()
                    for t in range(T):
                        ins = dve.bn_aggr(mv[u][:, t, :], stats[u][:, t, :])
                    ins.then_inc(S["moments"][u], 1)

                for name, u, n, back in steps:
                    g = it + back
                    if name == "mask":
                        dve.wait_ge(s_adj[u], g * 16 + 16)
                        link(dve.tensor_scalar(M3[u][:, :, :], edges[:, :, :], 0.0, -BIG, ALU.is_le, ALU.mult))
                        dve.tensor_copy(MN[u][:, :, :], M3[u][:, :, :]).then_inc(S["edges"][u], 1)
                    elif name == "norm":
                        if n == 0:
                            dve.wait_ge(s_x[u], g * 16 + 16)
                        elif n == 2:
                            dve.wait_ge(S["summed"][u], done(g, "summed", 0))
                        else:
                            key = ("gather", HEADS if n == 1 else ATT_L2, T - 1)
                            dve.wait_ge(freed(u, key), readout(g, key))
                        moments(lambda t: X[u][:, t, :], ("n", n))
                    elif name == "affine":
                        l = n // 2
                        key = ("gather", ATT_L1 + l, T - 1) if n % 2 == 0 else ("down", l, T - 1)
                        dve.wait_ge(freed(u, key), readout(g, key))
                        src = (lambda t: R1(u, t)) if n % 2 == 0 else (lambda t: Z[u][:, t, 0:D])
                        moments(src, ("a", n))
                        dve.wait_ge(S["rstd"][u], done(g, "rstd", ("a", n)))
                        for t in range(T):
                            at = dve.scalar_tensor_tensor(out=src(t), in0=src(t), scalar=mv[u][:, t, 0:1],
                                                          in1=g_row[:, n, :], op0=ALU.subtract, op1=ALU.mult)
                            if t == T - 1:
                                link(at)
                        for t in range(T):
                            ins = dve.scalar_tensor_tensor(out=HX[u][:, t, 0:D], in0=src(t),
                                                           scalar=norm_c[u][:, 1, t:t + 1],
                                                           in1=be_row[:, n, :], op0=ALU.mult, op1=ALU.add)
                        ins.then_inc(S["layered"][u], 1)
                    elif name in ("proj1", "proj2"):
                        key, dst = (("cols1",), ab1[u]) if name == "proj1" else (("cols2",), ab2[u])
                        w = dst.shape[2]
                        dve.wait_ge(s_mm[u], product(g, key))
                        dve.tensor_copy(dst[:, :, :], bank(u, key)[:, 0:T * w].rearrange("p (t c) -> p t c", c=w)
                                        ).then_inc(freed(u, key), 1)
                    elif name == "score":
                        if n < LAYERS and n > 0:
                            dve.wait_ge(S["layered"][u], done(g, "layered", 2 * n - 1))
                        else:
                            dve.wait_ge(S["normed"][u], done(g, "normed", 1 if n == 0 else 2))
                        pass_gate()
                        for t in range(T):
                            for c in range(2):
                                ins = dve.tensor_tensor_reduce(junk(u, t)[:, c * D:(c + 1) * D], HX[u][:, t, 0:D],
                                                               s_row[:, n, c, :], 1.0, 0.0, ALU.mult, ALU.add,
                                                               ab2[u][:, t, c:c + 1])
                        link(ins)
                        dve.tensor_scalar(ab2[u][:, :, 1], ab2[u][:, :, 1], s_bias[:, n:n + 1], None,
                                          ALU.add).then_inc(S["cols"][u], 1)
                    elif name == "max":
                        key = ("arow", n)
                        c = cols[u][:, n % 2]
                        if n in (0, ATT_L1, ATT_L2, HEADS):
                            dve.wait_ge(S["masks"][u], done(g, "masks", 0))
                        if 0 < n < HEADS:
                            dve.wait_ge(freed(u, ("hi", n - 1)), readout(g, ("hi", n - 1)))
                        dve.wait_ge(s_mm[u], product(g, key))
                        for t in range(T):
                            if t == 0:
                                pass_gate()
                            ins = dve.tensor_tensor_reduce(junk(u, t), bank(u, key)[:, :], masks(u, n)[1][:, t, :], 1.0,
                                                           -3e38, ALU.add, ALU.max, c[:, 0, t:t + 1])
                        ins.then_inc(freed(u, key), 1)
                        dve.wait_ge(freed(u, key), readout(g, key))
                        a, b = a_cols(u, n), b_cols(u, n)
                        link(dve.tensor_tensor(c[:, 1, :], c[:, 0, :], b, ALU.add))
                        link(dve.scalar_tensor_tensor(out=c[:, 2, :], in0=c[:, 1, :], scalar=SLOPE, in1=c[:, 1, :],
                                                      op0=ALU.mult, op1=ALU.max))
                        dve.tensor_tensor(c[:, 3, :], b, c[:, 2, :], ALU.subtract)
                        dve.tensor_scalar(a_low[u][:, n % 2, :], a, SLOPE, None, ALU.mult)
                        dve.scalar_tensor_tensor(out=c[:, 4, :], in0=b, scalar=SLOPE, in1=c[:, 2, :],
                                                 op0=ALU.mult, op1=ALU.subtract).then_inc(S["shift"][u], 1)
                    elif name == "weights":
                        lo, hi = ("lo", n), ("hi", n)
                        dve.wait_ge(s_mm[u], product(g, hi))
                        for t in range(T):
                            if t < T - 1:
                                dve.wait_ge(S["low"][u], done(g, "low", (n, t)))
                            else:
                                dve.wait_ge(freed(u, lo), readout(g, lo))
                            dve.scalar_tensor_tensor(out=Z[u][:, t, :], in0=bank(u, hi)[:, :],
                                                     scalar=a_cols(u, n)[:, t:t + 1], in1=LOW[u][:, t % 2, :],
                                                     op0=ALU.add, op1=ALU.max
                                                     ).then_inc(S["high"][u] if t < T - 1 else freed(u, hi), 1)
                    elif name == "gather":
                        width = HF if n < HEADS else D
                        if n == HEADS:
                            dve.wait_ge(S["xbias"][u], done(g, "xbias", 0))
                        at = [None] * T

                        def scale(t):
                            key = ("gather", n, t)
                            if n < HEADS:
                                dst, add = G[u][:, t, n * HF:(n + 1) * HF], b1row[:, n * HF:(n + 1) * HF]
                            elif n in (HEADS, ATT_L2):
                                dst = add = X[u][:, t, :]
                            else:
                                dst, add = R1(u, t), HX[u][:, t, 0:D]
                            dve.wait_ge(s_dve[u], at[t])
                            dve.scalar_tensor_tensor(out=dst, in0=bank(u, key)[:, 0:width], scalar=rden[u][:, t:t + 1],
                                                     in1=add, op0=ALU.mult, op1=ALU.add).then_inc(freed(u, key), 1)

                        for t in range(T):
                            key = ("gather", n, t)
                            dve.wait_ge(s_mm[u], product(g, key))
                            at[t] = take(dve.reciprocal(rden[u][:, t:t + 1], bank(u, key)[:, width:width + 1]))
                            if t:
                                scale(t - 1)
                        scale(T - 1)
                    elif name == "elu":
                        for t in range(T):
                            dve.wait_ge(S["elu_exp"][u], done(g, "elu_exp", t))
                            link(dve.tensor_scalar(Z[u][:, t, :], Z[u][:, t, :], 1.0, -1.0, ALU.min, ALU.add))
                            dve.scalar_tensor_tensor(out=G[u][:, t, :], in0=G[u][:, t, :], scalar=0.0,
                                                     in1=Z[u][:, t, :], op0=ALU.max, op1=ALU.add
                                                     ).then_inc(S["elu"][u], 1)
                    elif name == "down":
                        l, t = n
                        if t == 0:
                            dve.wait_ge(S["hbias"][u], done(g, "hbias", l))
                        key = ("down", l, t)
                        dve.wait_ge(s_mm[u], product(g, key))
                        dve.tensor_tensor(Z[u][:, t, 0:D], bank(u, key)[:, 0:D], HX[u][:, t, 0:D],
                                          ALU.add).then_inc(freed(u, key), 1)
                    elif name == "dotproj":
                        for t in range(T):
                            key = ("h", t)
                            dve.wait_ge(s_mm[u], product(g, key))
                            dve.tensor_tensor(HX[u][:, t, 0:D], bank(u, key)[:, 0:D], b3row[:, :],
                                              ALU.add).then_inc(freed(u, key), 1)
                    elif name == "dotscore":
                        c = dmax[u]
                        for t in range(T):
                            key = ("dots", t)
                            dve.wait_ge(s_mm[u], product(g, key))
                            pass_gate()
                            dve.tensor_tensor_reduce(Z[u][:, t, :], bank(u, key)[:, :], M3[u][:, t, :], 1.0, -3e38,
                                                     ALU.add, ALU.max, c[:, 0, t:t + 1]).then_inc(freed(u, key), 1)
                            dve.wait_ge(freed(u, key), readout(g, key))
                        link(dve.tensor_scalar(c[:, 1, :], c[:, 0, :], 1e9, 0.0, ALU.mult, ALU.min))
                        link(dve.tensor_tensor(c[:, 2, :], c[:, 1, :], c[:, 1, :], ALU.subtract))
                        dve.scalar_tensor_tensor(out=c[:, 3, :], in0=c[:, 0, :], scalar=-1.0, in1=c[:, 2, :],
                                                 op0=ALU.mult, op1=ALU.add).then_inc(S["dotmax"][u], 1)
                    elif name == "dotturn":
                        dve.wait_ge(S["dotexp"][u], done(g, "dotexp", 0))
                        link(dve.reciprocal(rden[u][:, :], dden[u][:, :]))
                    elif name == "dotout":
                        for t in range(T):
                            key = ("dotout", t)
                            dve.wait_ge(s_mm[u], product(g, key))
                            dve.tensor_scalar(Z[u][:, t, 0:D], bank(u, key)[:, 0:D], rden[u][:, t:t + 1], None,
                                              ALU.mult).then_inc(freed(u, key), 1)
                        for t in range(T):
                            dve.wait_ge(S["out_exp"][u], done(g, "out_exp", t))
                            e, y = Z[u][:, t, D:2 * D], Z[u][:, t, 0:D]
                            link(dve.tensor_scalar(e, e, 1.0, -1.0, ALU.min, ALU.add))
                            link(dve.scalar_tensor_tensor(out=y, in0=y, scalar=0.0, in1=e, op0=ALU.max,
                                                          op1=ALU.add))
                            ins = dve.tensor_tensor(X[u][:, t, :], X[u][:, t, :], y, ALU.add)
                        ins.then_inc(S["out"][u], 1)
                        assert links[u] == DVE_LINKS, links[u]
                        links[u] = gates[u] = 0

            run(FIRST_TURN, 0)
            with dve.Fori(1, TURNS) as it:
                run(TURN, it)
            run(LAST_TURN, TURNS)


POOL_LINKS = 1 + 2 * (4 + 2 * 3)
DVE_LINKS = 1 + (4 + 6) + 6 + 4 + 9 * 2 + 9 * 4 + 4 + 2 + 1 + 4 * 2

_INS = ["x", "adj", "L0_gnn_W1", "L0_gnn_att_src1", "L0_gnn_att_dst1", "L0_gnn_b1", "L0_gnn_W2",
        "L0_gnn_att_src2", "L0_gnn_att_dst2", "L0_gnn_b2", "L1_gnn_attn_w", "L1_gnn_attn_b", "L1_gnn_W1",
        "L1_gnn_b1", "L1_gnn_W2", "L1_gnn_b2", "L1_gnn_g1", "L1_gnn_beta1", "L1_gnn_g2", "L1_gnn_beta2",
        "L2_gnn_attn_w_src", "L2_gnn_attn_w_dst", "L2_gnn_attn_b", "L3_gnn_W", "L3_gnn_b", "L3_gnn_attn"]


def kernel(**inputs):
    import numpy as np
    import concourse.bacc as bacc
    from concourse.bass_utils import run_bass_kernel_spmd as run

    nc = bacc.Bacc("TRN2", target_bir_lowering=False, num_devices=1)
    arrays, args = {}, []
    for name in _INS + ["b3_by_part"]:
        a = np.asarray(inputs["L3_gnn_b" if name == "b3_by_part" else name])
        if name == "L1_gnn_b1":
            a = a.reshape(a.shape[0], -1, P).transpose(2, 0, 1)
        if name == "b3_by_part":
            a = a.reshape(-1, P).T
        if name == "L3_gnn_W":
            a = a.T
        a = np.ascontiguousarray(a)
        arrays[f"in_{name}"] = a
        args.append(nc.dram_tensor(f"in_{name}", a.shape, mybir.dt.from_np(a.dtype), kind="ExternalInput").ap())
    out = nc.dram_tensor("out", inputs["x"].shape, F32, kind="ExternalOutput").ap()
    gnn_kernel(nc, *args, out)
    r = run(nc, [arrays], core_ids=[0])
    return r.results[0]["out"]
```

```python
from contextlib import ExitStack

import concourse.bass as bass
from concourse import mybir

ALU = mybir.AluOpType
ACT = mybir.ActivationFunctionType
F32 = mybir.dt.float32
BF16 = mybir.dt.bfloat16
I32 = mybir.dt.int32

P = 128
UNITS = 2
BANKS = 4
BIG = 1e30
SLOPE = 0.2
EPS = 1e-5
HEADS = 4
FFN_PARTS = 4
ATT_L1, ATT_L2 = HEADS + 1, HEADS + 4


def steps_of():
    s = [("load", 0), ("mask", 0), ("moments", ("n", 0)), ("norm", 0), ("turn", 0), ("proj1", 0), ("max", 0)]
    for h in range(HEADS):
        s.append(("weights", h))
        if h + 1 < HEADS:
            s.append(("max", h + 1))
        if h:
            s.append(("elu", h - 1))
        s.append(("gather", h))
    s += [("elu", HEADS - 1), ("turn1", 0), ("proj2", 0), ("max", HEADS), ("weights", HEADS), ("gather", HEADS)]
    s += [("moments", ("n", 1)), ("norm", 1)]
    for l in range(3):
        a = ATT_L1 + l
        s += [("score", l), ("max", a), ("weights", a), ("gather", a)]
        s += [("moments", ("a", 2 * l)), ("affine", 2 * l), ("turn", 1 + l)]
        s += [("up", (l, i)) for i in range(FFN_PARTS)]
        s += [("down", (l, i)) for i in range(FFN_PARTS)]
        s += [("moments", ("a", 2 * l + 1)), ("affine", 2 * l + 1)]
    s += [("resid", 0), ("moments", ("n", 2)), ("norm", 2)]
    s += [("score", 3), ("max", ATT_L2), ("weights", ATT_L2), ("gather", ATT_L2)]
    s += [("moments", ("n", 3)), ("norm", 3), ("turn", 4), ("dotproj", 0), ("dotscore", 0), ("dotturn", 0)]
    s += [("dotout", 0), ("store", 0)]
    return s


BEHIND = 5
WHOSE_STEP = ("110001011100111000100011001101000101001010111001110110100010"
              "101000100111001010101100010011101011001011100101010101100101"
              "010010101000110111100010101110000111010000110101111011011001"
              "0101101001")


def interleave():
    steps = steps_of()
    at = [0, len(steps) - BEHIND]
    turn = []
    for u in map(int, WHOSE_STEP):
        name, n = steps[at[u] % len(steps)]
        turn.append((name, u, n, -1 if u and at[u] < len(steps) else 0))
        at[u] += 1
    assert at == [len(steps), 2 * len(steps) - BEHIND]
    return turn


TURN = interleave()
FIRST_TURN = [s for s in TURN if s[3] == 0]
LAST_TURN = [s for s in TURN if s[3] < 0]


def plan(T, KC, FC):
    groups, marks = [], {}

    def mark(name, *keys):
        marks.setdefault(name, []).extend(keys)

    for name, n in steps_of():
        if name == "mask":
            mark("edges", 0)
            mark("masks", 0)
            groups += [("maskT", c) for c in range(T)]
        elif name == "moments":
            mark("moments", n)
            mark("rstd", n)
        elif name == "norm":
            mark("normed", n)
            if n == 0:
                mark("xbias", 0)
        elif name == "affine":
            mark("layered", n)
        elif name == "turn":
            groups += [("turn", n, c) for c in range(KC)]
            if 1 <= n <= 3:
                mark("hbias", n - 1)
        elif name == "proj1":
            groups += [("cols1",)] + [("values1", t) for t in range(T)]
            mark("ones1", 0)
        elif name == "proj2":
            groups += [("values2", t) for t in range(T)]
        elif name == "score":
            mark("cols", n)
        elif name == "max":
            groups.append(("arow", n))
            mark("shift", n)
        elif name == "weights":
            groups += [("lo", n), ("hi", n)]
            for t in range(T):
                if t < T - 1:
                    mark("low", (n, t))
                    mark("high", (n, t))
                    mark("masked", (n, t))
                else:
                    mark("masked_last", n)
                mark("exp", (n, t))
        elif name == "gather":
            groups += [("gather", n, t) for t in range(T)]
        elif name == "elu":
            mark("elu_exp", n)
            mark("elu", n)
        elif name == "turn1":
            groups += [("turn1", c) for c in range(T)]
        elif name == "up":
            each = FC // FFN_PARTS
            groups += [("up", n[0], f) for f in range(n[1] * each, (n[1] + 1) * each)]
        elif name == "down":
            groups.append(("down", n[0], n[1]))
        elif name == "resid":
            mark("summed", 0)
        elif name == "dotproj":
            groups += [("hT", c) for c in range(KC)] + [("haT", c) for c in range(KC)]
            groups += [("h", i) for i in range(T // 2)]
        elif name == "dotscore":
            groups += [("dots", t) for t in range(T)]
            mark("dotmax", 0)
            mark("dotexp", 0)
        elif name == "dotturn":
            groups += [("probT", t) for t in range(T)]
        elif name == "dotout":
            groups += [("dotout", t) for t in range(T)]
            mark("out_exp", *range(T))
            mark("out", 0)
    return groups, marks


def gnn_kernel(nc, x, adj, w1, as1, ad1, b1, w2, as2, ad2, b2, aw, ab, fw1, fb1, fw2, fb2, g1, be1, g2, be2,
               sw, dw, sb2, w3t, attn3, b3_by_part, out):
    B, N, D = x.shape
    T = N // P
    KC = D // P
    HF = w1.shape[1] // HEADS
    D1 = HEADS * HF
    LAYERS, _, FF = fw1.shape
    FC = FF // P
    TURNS = B // UNITS
    assert HF == P and D1 == N and T == HEADS and FC == 2 * T

    groups, marks = plan(T, KC, FC)
    group_at = {g: i for i, g in enumerate(groups)}
    mark_at = {name: {k: i for i, k in enumerate(keys)} for name, keys in marks.items()}
    uses_of_bank = [len(range(b, len(groups), BANKS)) for b in range(BANKS)]

    with ExitStack() as ctx:
        def sb(name, shape, dt=F32):
            return ctx.enter_context(nc.sbuf_tensor(name, shape, dt))

        def sem(name):
            return ctx.enter_context(nc.semaphore(name))

        W1 = sb("W1", [P, KC, D1])
        W2 = sb("W2", [P, T, D + 2])
        FW1 = sb("FW1", [P, LAYERS, KC, FF])
        FW2 = sb("FW2", [P, LAYERS, FC, D])
        W3T = sb("W3T", [P, KC, D])
        A3 = sb("A3", [P, KC, D])
        b1row = sb("b1row", [P, D1])
        b2row = sb("b2row", [P, D])
        g_row = sb("g_row", [P, 2 * LAYERS, D])
        be_row = sb("be_row", [P, 2 * LAYERS, D])
        fb2row = sb("fb2row", [P, LAYERS, D])
        s_row = sb("s_row", [P, LAYERS + 1, 2, D])
        s_bias = sb("s_bias", [P, LAYERS + 1])
        fb1col = sb("fb1col", [P, LAYERS, FC])
        b3col = sb("b3col", [P, KC])
        wa1 = sb("wa1", [P, KC, 2 * HEADS])
        ident = sb("ident", [P, P])
        identb = sb("identb", [P, P], BF16)
        offdiag = sb("offdiag", [P, P], BF16)
        c_eps = sb("c_eps", [P, T])
        c_neg1 = sb("c_neg1", [P, T])
        c_half = sb("c_half", [P, T])
        edges = sb("edges", [P, T, N], I32)

        def per_unit(name, shape, dt=F32):
            return [sb(f"{name}{u}", shape, dt) for u in range(UNITS)]

        X = per_unit("X", [P, T, D])
        HX = per_unit("HX", [P, T, D + 1])
        HT = per_unit("HT", [P, KC, N])
        M3 = per_unit("M3", [P, T, N], BF16)
        MN = per_unit("MN", [P, T, N], BF16)
        MT = per_unit("MT", [P, T, N], BF16)
        LOW = per_unit("LOW", [P, 2, N])
        Z = per_unit("Z", [P, T, N])
        G = per_unit("G", [P, T, N])
        V1 = per_unit("V1", [P, T, HEADS * (HF + 1)])
        ab1 = per_unit("ab1", [P, T, 2 * HEADS])
        ab2 = per_unit("ab2", [P, T, 2])
        cols = per_unit("cols", [P, 2, 5, T])
        a_low = per_unit("a_low", [P, 2, T])
        stats = per_unit("stats", [P, T, 6])
        mv = per_unit("mv", [P, T, 2])
        norm_c = per_unit("norm_c", [P, 4, T])
        rden = per_unit("rden", [P, T])
        dmax = per_unit("dmax", [P, 4, T])
        dden = per_unit("dden", [P, T])

        gate = per_unit("gate", [P, 64])

        ring = [[ctx.enter_context(nc.psum_tensor(f"ring{u}{b}", [P, N], F32)) for b in range(BANKS)]
                for u in range(UNITS)]

        s_w0 = sem("block_0_weights_loaded")
        s_w = sem("other_weights_loaded")
        s_const = sem("constants_set")
        s_fold = sem("score_weights_folded")
        s_x = [sem(f"x_loaded{u}") for u in range(UNITS)]
        s_adj = [sem(f"adj_loaded{u}") for u in range(UNITS)]
        s_store = [sem(f"stored{u}") for u in range(UNITS)]
        s_mm = [sem(f"product_done{u}") for u in range(UNITS)]
        s_free = [[sem(f"bank_read{u}{b}") for b in range(BANKS)] for u in range(UNITS)]
        s_pre = sem("folding_step")
        s_dve = [sem(f"vector_step{u}") for u in range(UNITS)]
        s_pool = [sem(f"pool_step{u}") for u in range(UNITS)]
        S = {name: [sem(f"{name}_done{u}") for u in range(UNITS)] for name in marks}

        SEED = 1

        def bank(u, key):
            return ring[u][group_at[key] % BANKS]

        def freed(u, key):
            return s_free[u][group_at[key] % BANKS]

        def product(g, key):
            return g * len(groups) + group_at[key] + 1

        def readout(g, key):
            i = group_at[key]
            return SEED + g * uses_of_bank[i % BANKS] + i // BANKS + 1

        def done(g, name, key):
            return g * len(marks[name]) + mark_at[name][key] + 1

        def V1h(u, t, h):
            return V1[u][:, t, h * (HF + 1):(h + 1) * (HF + 1)]

        def H1T(u, c):
            return V1[u][:, :, :].rearrange("p t n -> p (t n)")[:, c * N:(c + 1) * N]

        def hidden(u, f):
            return G[u][:, f, :] if f < T else H1T(u, f - T)

        def R1(u, t):
            return G[u][:, :, :].rearrange("p t n -> p (t n)")[:, t * D:(t + 1) * D]

        def head(u, h):
            return G[u][:, :, h * HF:(h + 1) * HF]

        def elu_exp(u, h):
            return HT[u][:, h % 2, :].rearrange("p (t f) -> p t f", f=HF)

        def junk(u, t):
            return LOW[u][:, t // 2, :].bitcast(BF16)[:, (t % 2) * N:(t % 2 + 1) * N]

        def a_cols(u, n):
            return ab1[u][:, :, n] if n < HEADS else ab2[u][:, :, 0]

        def b_cols(u, n):
            return ab1[u][:, :, HEADS + n] if n < HEADS else ab2[u][:, :, 1]

        def masks(u, n):
            return (MN[u], MT[u]) if n <= HEADS else (MT[u], MN[u])

        def values(u, n, t):
            return V1h(u, t, n) if n < HEADS else HX[u][:, t, :]

        nodes = "b (t p) d -> b p t d"
        x_v, adj_v, out_v = (a.rearrange(nodes, p=P) for a in (x, adj, out))

        nc.disable_value_cache = True
        block = ctx.enter_context(nc.Block())
        first_loads = [
            (W1[:, :, :], w1.rearrange("(k p) n -> p k n", p=P)),
            (G[0][:, 0, :], as1.rearrange("h f -> (h f)").partition_broadcast(P)),
            (G[0][:, 1, :], ad1.rearrange("h f -> (h f)").partition_broadcast(P)),
            (G[0][:, 2, 0:D], as2.rearrange("h f -> (h f)").partition_broadcast(P)),
            (G[0][:, 2, D:2 * D], ad2.rearrange("h f -> (h f)").partition_broadcast(P)),
            (W2[:, :, 0:D], w2.rearrange("(k p) n -> p k n", p=P)),
            (b1row[:, :], b1.partition_broadcast(P)),
            (b2row[:, :], b2.partition_broadcast(P)),
        ]
        loads = [
            (s_bias[:, 0:LAYERS], ab.partition_broadcast(P)),
            (s_bias[:, LAYERS:LAYERS + 1], sb2.partition_broadcast(P)),
            (fb1col[:, :, :], fb1),
            (b3col[:, :], b3_by_part),
            (fb2row[:, :, :], fb2.partition_broadcast(P)),
            (s_row[:, LAYERS, 0, :], dw.partition_broadcast(P)),
            (s_row[:, LAYERS, 1, :], sw.partition_broadcast(P)),
            (W3T[:, :, :], w3t.rearrange("(k p) n -> p k n", p=P)),
            (A3[:, :, :], attn3.rearrange("(k p) n -> p k n", p=P)),
        ]
        for l in range(LAYERS):
            loads += [
                (FW1[:, l, :, :], fw1[l].rearrange("(k p) n -> p k n", p=P)),
                (FW2[:, l, :, :], fw2[l].rearrange("(k p) n -> p k n", p=P)),
                (g_row[:, 2 * l, :], g1[l].partition_broadcast(P)),
                (g_row[:, 2 * l + 1, :], g2[l].partition_broadcast(P)),
                (be_row[:, 2 * l, :], be1[l].partition_broadcast(P)),
                (be_row[:, 2 * l + 1, :], be2[l].partition_broadcast(P)),
                (s_row[:, l, 1, :], aw[l, 0:D].partition_broadcast(P)),
                (s_row[:, l, 0, :], aw[l, D:2 * D].partition_broadcast(P)),
            ]

        def block_1_begins(steps, name, n):
            return steps is FIRST_TURN and (name, n) == ("norm", 1)

        @block.sync
        def _(sp):
            for u in range(UNITS):
                for free in s_free[u]:
                    sp.sem_inc(free, SEED)
                sp.sem_inc(s_store[u], 16 * SEED)
            for dst, src in first_loads:
                sp.dma_start(dst, src).then_inc(s_w0, 16)

            def run(steps, it):
                for name, u, n, back in steps:
                    g = it + back
                    if name == "load":
                        if u == 1 or steps is TURN:
                            sp.wait_ge(S["edges"][1 - u], g + u)
                        sp.dma_start(edges[:, :, :], adj_v[g * UNITS + u]).then_inc(s_adj[u], 16)
                        sp.dma_start(X[u][:, :, :], x_v[g * UNITS + u]).then_inc(s_x[u], 16)
                        if steps is FIRST_TURN and u == 0:
                            for dst, src in loads:
                                sp.dma_start(dst, src).then_inc(s_w, 16)
                    elif name == "store":
                        sp.wait_ge(S["out"][u], done(g, "out", 0))
                        sp.dma_start(out_v[g * UNITS + u], Z[u][:, :, 0:D]).then_inc(s_store[u], 16)

            run(FIRST_TURN, 0)
            with sp.Fori(1, TURNS) as it:
                run(TURN, it)
            run(LAST_TURN, TURNS)
            for u in range(UNITS):
                sp.wait_ge(s_store[u], 16 * SEED + 16 * TURNS)

        @block.gpsimd
        def _(pool):
            pool.memset(ident[:, :], 0.0)
            pool.memset(identb[:, :], 0.0)
            pool.memset(offdiag[:, :], 1.0)
            pool.memset(c_eps[:, :], EPS)
            pool.memset(c_neg1[:, :], -1.0)
            for u in range(UNITS):
                pool.memset(HX[u][:, :, D:D + 1], 1.0)
            pool.memset(c_half[:, :], -0.5).then_inc(s_const, 1)
            pool.wait_ge(s_const, 1)
            for m, v in ((ident, 1.0), (identb, 1.0), (offdiag, 0.0)):
                pool.affine_select(out=m[:, :], in_=m[:, :], compare_op=ALU.not_equal, fill=v, base=0,
                                   pattern=[[-1, P]], channel_multiplier=1).then_inc(s_const, 1)
            pool.wait_ge(s_const, 4)
            pool.wait_ge(s_w0, 16 * len(first_loads))
            links = [0] * UNITS

            def run(steps, it):
                def link(ins):
                    links[u] += 1
                    ins.then_inc(s_pool[u], 1)
                    pool.wait_ge(s_pool[u], g * POOL_LINKS + links[u])

                for name, u, n, back in steps:
                    g = it + back
                    if block_1_begins(steps, name, n):
                        pool.wait_ge(s_w, 16 * len(loads))
                    if name == "mask":
                        pool.wait_ge(S["edges"][u], done(g, "edges", 0))
                        for t in range(T):
                            d = MN[u][:, t, t * P:(t + 1) * P]
                            pool.tensor_tensor(d, d, offdiag[:, :], ALU.mult)
                        for t in range(T):
                            pool.wait_ge(freed(u, ("maskT", t)), readout(g, ("maskT", t)))
                            d = MT[u][:, t, t * P:(t + 1) * P]
                            ins = pool.tensor_tensor(d, d, offdiag[:, :], ALU.mult)
                        ins.then_inc(S["masks"][u], 1)
                    elif name == "moments":
                        pool.wait_ge(S["moments"][u], done(g, "moments", n))
                        c = norm_c[u]
                        pool.tensor_tensor(c[:, 2, :], mv[u][:, :, 0], c_neg1[:, :], ALU.mult)
                        link(pool.tensor_tensor(c[:, 0, :], mv[u][:, :, 1], c_eps[:, :], ALU.add))
                        link(pool.tensor_tensor(c[:, 1, :], c[:, 0, :], c_half[:, :], ALU.pow))
                        pool.tensor_tensor(c[:, 3, :], c[:, 2, :], c[:, 1, :], ALU.mult).then_inc(S["rstd"][u], 1)
                    elif name == "norm" and n == 0:
                        pool.wait_ge(S["normed"][u], done(g, "normed", 0))
                        for t in range(T):
                            ins = pool.tensor_tensor(X[u][:, t, :], X[u][:, t, :], b2row[:, :], ALU.add)
                        ins.then_inc(S["xbias"][u], 1)
                    elif name == "proj1":
                        ones = V1[u][:, :, :].rearrange("p t (h f) -> p t h f", h=HEADS)[:, :, :, HF]
                        pool.memset(ones, 1.0).then_inc(S["ones1"][u], 1)
                    elif name == "turn" and 1 <= n <= LAYERS:
                        pool.wait_ge(s_mm[u], product(g, ("turn", n, KC - 1)))
                        for t in range(T):
                            ins = pool.tensor_tensor(HX[u][:, t, 0:D], HX[u][:, t, 0:D], fb2row[:, n - 1, :],
                                                     ALU.add)
                        ins.then_inc(S["hbias"][u], 1)
                    elif name == "weights":
                        for t in range(T - 1):
                            pool.wait_ge(S["high"][u], done(g, "high", (n, t)))
                            pool.tensor_tensor(Z[u][:, t, :], Z[u][:, t, :], masks(u, n)[0][:, t, :],
                                               ALU.add).then_inc(S["masked"][u], 1)
                    elif name == "resid":
                        pool.wait_ge(S["layered"][u], done(g, "layered", 2 * LAYERS - 1))
                        link(pool.tensor_tensor(X[u][:, 0:T // 2, :], X[u][:, 0:T // 2, :],
                                                HX[u][:, 0:T // 2, 0:D], ALU.add))
                        pool.tensor_tensor(X[u][:, T // 2:T, :], X[u][:, T // 2:T, :],
                                           HX[u][:, T // 2:T, 0:D], ALU.add).then_inc(S["summed"][u], 1)
                    elif name == "store":
                        assert links[u] == POOL_LINKS, links[u]
                        links[u] = 0

            run(FIRST_TURN, 0)
            with pool.Fori(1, TURNS) as it:
                run(TURN, it)
            run(LAST_TURN, TURNS)

        @block.scalar
        def _(act):
            def run(steps, it):
                def read(dst, src_of, key, func=ACT.Copy, **kw):
                    act.wait_ge(s_mm[u], product(g, key))
                    act.activation(dst, src_of(bank(u, key)), func, **kw).then_inc(freed(u, key), 1)

                for name, u, n, back in steps:
                    g = it + back
                    if block_1_begins(steps, name, n):
                        act.wait_ge(s_w, 16 * len(loads))
                    if name == "mask":
                        for c in range(T):
                            read(MT[u][:, c, :], lambda b: b[:, :].bitcast(BF16)[:, 0:N], ("maskT", c))
                    elif name == "norm":
                        act.wait_ge(S["rstd"][u], done(g, "rstd", ("n", n)))
                        for t in range(T):
                            ins = act.activation(HX[u][:, t, 0:D], X[u][:, t, :], ACT.Relu,
                                                 bias=norm_c[u][:, 3, t:t + 1], scale=norm_c[u][:, 1, t:t + 1])
                        ins.then_inc(S["normed"][u], 1)
                    elif name == "turn":
                        for c in range(KC):
                            read(HT[u][:, c, :], lambda b: b[:, :], ("turn", n, c))
                    elif name == "proj1":
                        act.wait_ge(S["ones1"][u], done(g, "ones1", 0))
                        for t in range(T):
                            v = V1[u][:, t, :].rearrange("p (h f) -> p h f", h=HEADS)[:, :, 0:HF]
                            read(v, lambda b: b[:, :].rearrange("p (h f) -> p h f", h=HEADS), ("values1", t))
                    elif name == "proj2":
                        for t in range(T):
                            key = ("values2", t)
                            act.wait_ge(s_mm[u], product(g, key))
                            act.activation(HX[u][:, t, 0:D], bank(u, key)[:, 0:D], ACT.Copy)
                            act.activation(ab2[u][:, t, :], bank(u, key)[:, D:D + 2],
                                           ACT.Copy).then_inc(freed(u, key), 1)
                    elif name == "weights":
                        def low(t):
                            if t == 0:
                                act.wait_ge(s_mm[u], product(g, ("lo", n)))
                            if t >= 2:
                                act.wait_ge(S["high"][u], done(g, "high", (n, t - 2)))
                            last = t == T - 1
                            act.activation(LOW[u][:, t % 2, :], bank(u, ("lo", n))[:, :], ACT.Identity,
                                           bias=a_low[u][:, n % 2, t:t + 1]
                                           ).then_inc(freed(u, ("lo", n)) if last else S["low"][u], 1)

                        def exp(t):
                            if t < T - 1:
                                act.wait_ge(S["masked"][u], done(g, "masked", (n, t)))
                            else:
                                act.wait_ge(S["masked_last"][u], done(g, "masked_last", n))
                            act.activation(Z[u][:, t, :], Z[u][:, t, :], ACT.Exp).then_inc(S["exp"][u], 1)

                        low(0)
                        low(1)
                        for t in range(2, T):
                            low(t)
                            exp(t - 2)
                        exp(T - 2)
                        exp(T - 1)
                    elif name == "elu":
                        key = ("gather", n, T - 1)
                        act.wait_ge(freed(u, key), readout(g, key))
                        act.activation(elu_exp(u, n), head(u, n), ACT.Exp).then_inc(S["elu_exp"][u], 1)
                    elif name == "turn1":
                        for c in range(T):
                            read(H1T(u, c), lambda b: b[:, :], ("turn1", c))
                    elif name == "up":
                        l, part = n
                        for f in range(part * FC // FFN_PARTS, (part + 1) * FC // FFN_PARTS):
                            read(hidden(u, f), lambda b: b[:, :], ("up", l, f), ACT.Gelu,
                                 bias=fb1col[:, l, f:f + 1])
                    elif name == "dotproj":
                        for c in range(KC):
                            read(G[u][:, c, :], lambda b: b[:, :], ("hT", c), ACT.Identity,
                                 bias=b3col[:, c:c + 1])
                        for c in range(KC):
                            read(G[u][:, KC + c, :], lambda b: b[:, :], ("haT", c))
                    elif name == "dotscore":
                        act.wait_ge(S["dotmax"][u], done(g, "dotmax", 0))
                        for t in range(T):
                            ins = act.activation(Z[u][:, t, :], Z[u][:, t, :], ACT.Exp,
                                                 bias=dmax[u][:, 3, t:t + 1], accum_out=dden[u][:, t:t + 1])
                        ins.then_inc(S["dotexp"][u], 1)
                    elif name == "dotturn":
                        for t in range(T):
                            read(G[u][:, t, :], lambda b: b[:, :], ("probT", t))
                    elif name == "dotout":
                        for t in range(T):
                            key = ("dotout", t)
                            act.wait_ge(freed(u, key), readout(g, key))
                            act.activation(Z[u][:, t, D:2 * D], Z[u][:, t, 0:D],
                                           ACT.Exp).then_inc(S["out_exp"][u], 1)

            run(FIRST_TURN, 0)
            with act.Fori(1, TURNS) as it:
                run(TURN, it)
            run(LAST_TURN, TURNS)

        @block.tensor
        def _(pe):
            pe.wait_ge(s_const, 4)
            seen = [[-1] * BANKS for _ in range(UNITS)]

            def run(steps, it):
                def begin(key):
                    b, use = group_at[key] % BANKS, group_at[key] // BANKS
                    if use > seen[u][b]:
                        seen[u][b] = use
                        pe.wait_ge(freed(u, key), readout(g, key) - 1)
                    return bank(u, key)

                def after(key):
                    b, use = group_at[key] % BANKS, group_at[key] // BANKS
                    if use + 1 > seen[u][b]:
                        seen[u][b] = use + 1
                        pe.wait_ge(freed(u, key), readout(g, key))

                def spread(dst, col):
                    for t in range(T):
                        ins = pe.matmul(dst[:, t * P:(t + 1) * P], col[:, t:t + 1].broadcast_to([P, P]),
                                        ident[:, :], start=True, stop=True)
                    return ins

                def transpose4(key, src):
                    b = begin(key)
                    for t in range(T):
                        ins = pe.transpose(b[:, t * P:(t + 1) * P], src(t), ident[:, :])
                    ins.then_inc(s_mm[u], 1)

                def product_of(key, width, lhs, rhs, chunks):
                    b = begin(key)
                    for k in range(chunks):
                        ins = pe.matmul(b[:, 0:width], lhs(k), rhs(k), start=(k == 0), stop=(k == chunks - 1))
                    ins.then_inc(s_mm[u], 1)

                for name, u, n, back in steps:
                    g = it + back
                    if block_1_begins(steps, name, n):
                        pe.wait_ge(s_w, 16 * len(loads))
                    if name == "mask":
                        pe.wait_ge(S["edges"][u], done(g, "edges", 0))
                        for c in range(T):
                            b = begin(("maskT", c))[:, :].bitcast(BF16)
                            for t in range(T):
                                ins = pe.transpose(b[:, t * P:(t + 1) * P], M3[u][:, t, c * P:(c + 1) * P],
                                                   identb[:, :])
                            ins.then_inc(s_mm[u], 1)
                    elif name == "turn":
                        if n in (0, 4):
                            pe.wait_ge(S["normed"][u], done(g, "normed", 0 if n == 0 else 3))
                        else:
                            pe.wait_ge(S["layered"][u], done(g, "layered", 2 * (n - 1)))
                        for c in range(KC):
                            transpose4(("turn", n, c), lambda t: HX[u][:, t, c * P:(c + 1) * P])
                    elif name == "proj1":
                        if steps is FIRST_TURN:
                            pe.wait_ge(s_w0, 16 * len(first_loads))
                            pe.wait_ge(s_fold, 1)
                        for c in range(KC):
                            after(("turn", 0, c))
                        b = begin(("cols1",))
                        for t in range(T):
                            for k in range(KC):
                                ins = pe.matmul(b[:, t * 2 * HEADS:(t + 1) * 2 * HEADS],
                                                HT[u][:, k, t * P:(t + 1) * P], wa1[:, k, :],
                                                start=(k == 0), stop=(k == KC - 1))
                        ins.then_inc(s_mm[u], 1)
                        for t in range(T):
                            product_of(("values1", t), D1, lambda k: HT[u][:, k, t * P:(t + 1) * P],
                                       lambda k: W1[:, k, :], KC)
                    elif name == "proj2":
                        for c in range(T):
                            after(("turn1", c))
                        for t in range(T):
                            product_of(("values2", t), D + 2, lambda k: H1T(u, k)[:, t * P:(t + 1) * P],
                                       lambda k: W2[:, k, :], T)
                    elif name == "max":
                        if n < HEADS:
                            after(("cols1",))
                        elif n == HEADS:
                            for t in range(T):
                                after(("values2", t))
                        else:
                            pe.wait_ge(S["cols"][u], done(g, "cols", n - ATT_L1))
                        spread(begin(("arow", n)), a_cols(u, n)).then_inc(s_mm[u], 1)
                    elif name == "weights":
                        pe.wait_ge(S["shift"][u], done(g, "shift", n))
                        spread(begin(("lo", n)), cols[u][:, n % 2, 4, :]).then_inc(s_mm[u], 1)
                        spread(begin(("hi", n)), cols[u][:, n % 2, 3, :]).then_inc(s_mm[u], 1)
                    elif name == "gather":
                        if n < HEADS:
                            for t in range(T):
                                after(("values1", t))
                        if n == HEADS:
                            for t in range(T):
                                after(("values2", t))
                        width = (HF if n < HEADS else D) + 1
                        early = (0, 1)
                        into = [begin(("gather", n, t)) for t in early]
                        for s in range(T):
                            pe.wait_ge(S["exp"][u], done(g, "exp", (n, s)))
                            for t in early:
                                ins = pe.matmul(into[t][:, 0:width], Z[u][:, s, t * P:(t + 1) * P],
                                                values(u, n, s), start=(s == 0), stop=(s == T - 1))
                                if s == T - 1:
                                    ins.then_inc(s_mm[u], 1)
                        for t in range(len(early), T):
                            product_of(("gather", n, t), width, lambda s: Z[u][:, s, t * P:(t + 1) * P],
                                       lambda s: values(u, n, s), T)
                    elif name == "turn1":
                        for c in range(T):
                            pe.wait_ge(S["elu"][u], done(g, "elu", c))
                            transpose4(("turn1", c), lambda t: G[u][:, t, c * P:(c + 1) * P])
                    elif name == "up":
                        l, part = n
                        if part == 0:
                            for c in range(KC):
                                after(("turn", l + 1, c))
                        for f in range(part * FC // FFN_PARTS, (part + 1) * FC // FFN_PARTS):
                            product_of(("up", l, f), N, lambda k: FW1[:, l, k, f * P:(f + 1) * P],
                                       lambda k: HT[u][:, k, :], KC)
                    elif name == "down":
                        l, t = n
                        if t == 0:
                            for f in reversed(range(FC)):
                                after(("up", l, f))
                        product_of(("down", l, t), D, lambda k: hidden(u, k)[:, t * P:(t + 1) * P],
                                   lambda k: FW2[:, l, k, :], FC)
                    elif name == "dotproj":
                        for c in range(KC):
                            after(("turn", 4, c))
                        for c in range(KC):
                            product_of(("hT", c), N, lambda k: W3T[:, k, c * P:(c + 1) * P],
                                       lambda k: HT[u][:, k, :], KC)
                        for c in range(KC):
                            after(("hT", c))
                        for c in range(KC):
                            product_of(("haT", c), N, lambda k: A3[:, k, c * P:(c + 1) * P],
                                       lambda k: G[u][:, k, :], KC)
                        for i in range(T // 2):
                            b = begin(("h", i))
                            for t in (2 * i, 2 * i + 1):
                                for c in range(KC):
                                    ins = pe.transpose(b[:, (t % 2) * D + c * P:(t % 2) * D + (c + 1) * P],
                                                       G[u][:, c, t * P:(t + 1) * P], ident[:, :])
                            ins.then_inc(s_mm[u], 1)
                    elif name == "dotscore":
                        for c in range(KC):
                            after(("haT", c))
                        for t in range(T):
                            product_of(("dots", t), N, lambda k: G[u][:, KC + k, t * P:(t + 1) * P],
                                       lambda k: G[u][:, k, :], KC)
                    elif name == "dotturn":
                        pe.wait_ge(S["dotexp"][u], done(g, "dotexp", 0))
                        for c in range(T):
                            transpose4(("probT", c), lambda t: Z[u][:, t, c * P:(c + 1) * P])
                    elif name == "dotout":
                        for i in range(T // 2):
                            after(("h", i))
                        for t in range(T):
                            after(("probT", t))
                        for t in range(T):
                            product_of(("dotout", t), D, lambda k: G[u][:, k, t * P:(t + 1) * P],
                                       lambda k: HX[u][:, k, 0:D], T)
                        seen[u] = [-1] * BANKS

            run(FIRST_TURN, 0)
            with pe.Fori(1, TURNS) as it:
                run(TURN, it)
            run(LAST_TURN, TURNS)

        @block.vector
        def _(dve):
            dve.wait_ge(s_w0, 16 * len(first_loads))
            for k in range(KC):
                for c in range(2 * HEADS):
                    h = c % HEADS
                    dve.tensor_tensor_reduce(junk(0, 0)[:, 0:HF], W1[:, k, h * HF:(h + 1) * HF],
                                             G[0][:, c // HEADS, h * HF:(h + 1) * HF], 1.0, 0.0, ALU.mult,
                                             ALU.add, wa1[:, k, c:c + 1]).then_inc(s_pre, 1)
                    dve.wait_ge(s_pre, k * 2 * HEADS + c + 1)
            for k in range(T):
                for c in range(2):
                    dve.tensor_tensor_reduce(junk(0, 0)[:, 0:D], W2[:, k, 0:D], G[0][:, 2, c * D:(c + 1) * D], 1.0, 0.0,
                                             ALU.mult, ALU.add, W2[:, k, D + c:D + c + 1]).then_inc(s_pre, 1)
                    dve.wait_ge(s_pre, KC * 2 * HEADS + k * 2 + c + 1)
            dve.memset(gate[0][:, :], 0.0).then_inc(s_fold, 1)
            dve.wait_ge(s_fold, 1)
            links = [0] * UNITS
            gates = [0] * UNITS
            measured = [0] * UNITS

            def run(steps, it):
                def take(ins):
                    links[u] += 1
                    ins.then_inc(s_dve[u], 1)
                    return g * DVE_LINKS + links[u]

                def link(ins):
                    dve.wait_ge(s_dve[u], take(ins))

                def pass_gate():
                    dve.memset(gate[u][:, gates[u]:gates[u] + 1], 0.0)
                    gates[u] += 1

                def measure(t, src):
                    ins = dve.bn_stats(stats[u][:, t, :], src)
                    if t == T - 1:
                        take(ins)
                        measured[u] = links[u]

                for name, u, n, back in steps:
                    g = it + back
                    if block_1_begins(steps, name, n):
                        dve.wait_ge(s_w, 16 * len(loads))
                    if name == "mask":
                        dve.wait_ge(s_adj[u], g * 16 + 16)
                        link(dve.tensor_scalar(M3[u][:, :, :], edges[:, :, :], 0.0, -BIG, ALU.is_le, ALU.mult))
                        dve.tensor_copy(MN[u][:, :, :], M3[u][:, :, :]).then_inc(S["edges"][u], 1)
                    elif name == "moments":
                        if n in (("n", 0), ("n", 2)):
                            if n == ("n", 0):
                                dve.wait_ge(s_x[u], g * 16 + 16)
                            else:
                                dve.wait_ge(S["summed"][u], done(g, "summed", 0))
                            for t in range(T):
                                measure(t, X[u][:, t, :])
                        dve.wait_ge(s_dve[u], g * DVE_LINKS + measured[u])
                        pass_gate()
                        for t in range(T):
                            ins = dve.bn_aggr(mv[u][:, t, :], stats[u][:, t, :])
                        ins.then_inc(S["moments"][u], 1)
                    elif name == "affine":
                        src = (lambda t: R1(u, t)) if n % 2 == 0 else (lambda t: Z[u][:, t, 0:D])
                        dve.wait_ge(S["rstd"][u], done(g, "rstd", ("a", n)))
                        for t in range(T):
                            at = dve.scalar_tensor_tensor(out=src(t), in0=src(t), scalar=mv[u][:, t, 0:1],
                                                          in1=g_row[:, n, :], op0=ALU.subtract, op1=ALU.mult)
                            if t == T - 1:
                                link(at)
                        for t in range(T):
                            ins = dve.scalar_tensor_tensor(out=HX[u][:, t, 0:D], in0=src(t),
                                                           scalar=norm_c[u][:, 1, t:t + 1],
                                                           in1=be_row[:, n, :], op0=ALU.mult, op1=ALU.add)
                        ins.then_inc(S["layered"][u], 1)
                    elif name == "proj1":
                        key, dst, w = ("cols1",), ab1[u], 2 * HEADS
                        dve.wait_ge(s_mm[u], product(g, key))
                        dve.tensor_copy(dst[:, :, :], bank(u, key)[:, 0:T * w].rearrange("p (t c) -> p t c", c=w)
                                        ).then_inc(freed(u, key), 1)
                    elif name == "score":
                        if n < LAYERS and n > 0:
                            dve.wait_ge(S["layered"][u], done(g, "layered", 2 * n - 1))
                        else:
                            dve.wait_ge(S["normed"][u], done(g, "normed", 1 if n == 0 else 2))
                        pass_gate()
                        for t in range(T):
                            for c in range(2):
                                ins = dve.tensor_tensor_reduce(junk(u, t)[:, c * D:(c + 1) * D], HX[u][:, t, 0:D],
                                                               s_row[:, n, c, :], 1.0, 0.0, ALU.mult, ALU.add,
                                                               ab2[u][:, t, c:c + 1])
                        link(ins)
                        dve.tensor_scalar(ab2[u][:, :, 1], ab2[u][:, :, 1], s_bias[:, n:n + 1], None,
                                          ALU.add).then_inc(S["cols"][u], 1)
                    elif name == "max":
                        key = ("arow", n)
                        c = cols[u][:, n % 2]
                        if n in (0, ATT_L1, ATT_L2, HEADS):
                            dve.wait_ge(S["masks"][u], done(g, "masks", 0))
                        if 0 < n < HEADS:
                            dve.wait_ge(freed(u, ("hi", n - 1)), readout(g, ("hi", n - 1)))
                        dve.wait_ge(s_mm[u], product(g, key))
                        for t in range(T):
                            if t == 0:
                                pass_gate()
                            ins = dve.tensor_tensor_reduce(junk(u, t), bank(u, key)[:, :], masks(u, n)[1][:, t, :], 1.0,
                                                           -3e38, ALU.add, ALU.max, c[:, 0, t:t + 1])
                        ins.then_inc(freed(u, key), 1)
                        dve.wait_ge(freed(u, key), readout(g, key))
                        a, b = a_cols(u, n), b_cols(u, n)
                        link(dve.tensor_tensor(c[:, 1, :], c[:, 0, :], b, ALU.add))
                        link(dve.scalar_tensor_tensor(out=c[:, 2, :], in0=c[:, 1, :], scalar=SLOPE, in1=c[:, 1, :],
                                                      op0=ALU.mult, op1=ALU.max))
                        dve.tensor_tensor(c[:, 3, :], b, c[:, 2, :], ALU.subtract)
                        dve.tensor_scalar(a_low[u][:, n % 2, :], a, SLOPE, None, ALU.mult)
                        dve.scalar_tensor_tensor(out=c[:, 4, :], in0=b, scalar=SLOPE, in1=c[:, 2, :],
                                                 op0=ALU.mult, op1=ALU.subtract).then_inc(S["shift"][u], 1)
                    elif name == "weights":
                        lo, hi = ("lo", n), ("hi", n)
                        if n == 0:
                            dve.wait_ge(s_store[u], 16 * SEED + g * 16)
                        dve.wait_ge(s_mm[u], product(g, hi))
                        for t in range(T):
                            if t < T - 1:
                                dve.wait_ge(S["low"][u], done(g, "low", (n, t)))
                            else:
                                dve.wait_ge(freed(u, lo), readout(g, lo))
                            dve.scalar_tensor_tensor(out=Z[u][:, t, :], in0=bank(u, hi)[:, :],
                                                     scalar=a_cols(u, n)[:, t:t + 1], in1=LOW[u][:, t % 2, :],
                                                     op0=ALU.add, op1=ALU.max
                                                     ).then_inc(S["high"][u] if t < T - 1 else freed(u, hi), 1)
                        dve.wait_ge(freed(u, hi), readout(g, hi))
                        dve.tensor_tensor(Z[u][:, T - 1, :], Z[u][:, T - 1, :], masks(u, n)[0][:, T - 1, :],
                                          ALU.add).then_inc(S["masked_last"][u], 1)
                    elif name == "gather":
                        width = HF if n < HEADS else D
                        if n == HEADS:
                            dve.wait_ge(S["xbias"][u], done(g, "xbias", 0))
                        at = [None] * T

                        def place(t):
                            if n < HEADS:
                                return G[u][:, t, n * HF:(n + 1) * HF], b1row[:, n * HF:(n + 1) * HF]
                            if n in (HEADS, ATT_L2):
                                return X[u][:, t, :], X[u][:, t, :]
                            return R1(u, t), HX[u][:, t, 0:D]

                        def scale(t):
                            key = ("gather", n, t)
                            dst, add = place(t)
                            dve.wait_ge(s_dve[u], at[t])
                            dve.scalar_tensor_tensor(out=dst, in0=bank(u, key)[:, 0:width], scalar=rden[u][:, t:t + 1],
                                                     in1=add, op0=ALU.mult, op1=ALU.add).then_inc(freed(u, key), 1)

                        def check(t):
                            dve.wait_ge(freed(u, ("gather", n, t)), readout(g, ("gather", n, t)))
                            measure(t, place(t)[0])

                        for t in range(T):
                            key = ("gather", n, t)
                            dve.wait_ge(s_mm[u], product(g, key))
                            at[t] = take(dve.reciprocal(rden[u][:, t:t + 1], bank(u, key)[:, width:width + 1]))
                            if t:
                                scale(t - 1)
                            if t >= 2 and n >= HEADS:
                                check(t - 2)
                        scale(T - 1)
                        if n >= HEADS:
                            check(T - 2)
                            check(T - 1)
                    elif name == "elu":
                        dve.wait_ge(S["elu_exp"][u], done(g, "elu_exp", n))
                        e, y = elu_exp(u, n), head(u, n)
                        link(dve.tensor_scalar(e, e, 1.0, -1.0, ALU.min, ALU.add))
                        dve.scalar_tensor_tensor(out=y, in0=y, scalar=0.0, in1=e, op0=ALU.max,
                                                 op1=ALU.add).then_inc(S["elu"][u], 1)
                    elif name == "down":
                        l, t = n
                        if t == 0:
                            dve.wait_ge(S["hbias"][u], done(g, "hbias", l))
                        key = ("down", l, t)
                        dve.wait_ge(s_mm[u], product(g, key))
                        dve.tensor_tensor(Z[u][:, t, 0:D], bank(u, key)[:, 0:D], HX[u][:, t, 0:D],
                                          ALU.add).then_inc(freed(u, key), 1)
                        dve.wait_ge(freed(u, key), readout(g, key))
                        measure(t, Z[u][:, t, 0:D])
                    elif name == "dotproj":
                        for i in range(T // 2):
                            key = ("h", i)
                            dve.wait_ge(s_mm[u], product(g, key))
                            dve.tensor_copy(HX[u][:, 2 * i:2 * i + 2, 0:D],
                                            bank(u, key)[:, :].rearrange("p (t d) -> p t d", d=D)
                                            ).then_inc(freed(u, key), 1)
                    elif name == "dotscore":
                        c = dmax[u]
                        for t in range(T):
                            key = ("dots", t)
                            dve.wait_ge(s_mm[u], product(g, key))
                            pass_gate()
                            dve.tensor_tensor_reduce(Z[u][:, t, :], bank(u, key)[:, :], M3[u][:, t, :], 1.0, -3e38,
                                                     ALU.add, ALU.max, c[:, 0, t:t + 1]).then_inc(freed(u, key), 1)
                            dve.wait_ge(freed(u, key), readout(g, key))
                        link(dve.tensor_scalar(c[:, 1, :], c[:, 0, :], 1e9, 0.0, ALU.mult, ALU.min))
                        link(dve.tensor_tensor(c[:, 2, :], c[:, 1, :], c[:, 1, :], ALU.subtract))
                        dve.scalar_tensor_tensor(out=c[:, 3, :], in0=c[:, 0, :], scalar=-1.0, in1=c[:, 2, :],
                                                 op0=ALU.mult, op1=ALU.add).then_inc(S["dotmax"][u], 1)
                    elif name == "dotturn":
                        dve.wait_ge(S["dotexp"][u], done(g, "dotexp", 0))
                        link(dve.reciprocal(rden[u][:, :], dden[u][:, :]))
                    elif name == "dotout":
                        for t in range(T):
                            key = ("dotout", t)
                            dve.wait_ge(s_mm[u], product(g, key))
                            dve.tensor_scalar(Z[u][:, t, 0:D], bank(u, key)[:, 0:D], rden[u][:, t:t + 1], None,
                                              ALU.mult).then_inc(freed(u, key), 1)
                        for t in range(T):
                            dve.wait_ge(S["out_exp"][u], done(g, "out_exp", t))
                            e, y = Z[u][:, t, D:2 * D], Z[u][:, t, 0:D]
                            link(dve.tensor_scalar(e, e, 1.0, -1.0, ALU.min, ALU.add))
                            link(dve.scalar_tensor_tensor(out=y, in0=y, scalar=0.0, in1=e, op0=ALU.max,
                                                          op1=ALU.add))
                            ins = dve.tensor_tensor(y, X[u][:, t, :], y, ALU.add)
                        ins.then_inc(S["out"][u], 1)
                        assert links[u] == DVE_LINKS, links[u]
                        links[u] = gates[u] = 0

            run(FIRST_TURN, 0)
            with dve.Fori(1, TURNS) as it:
                run(TURN, it)
            run(LAST_TURN, TURNS)


POOL_LINKS = 1 + 2 * (4 + 2 * 3)
DVE_LINKS = 1 + (4 + 6) + 6 + 4 + 9 * 2 + 9 * 4 + 4 + 2 + 1 + 4 * 2

_INS = ["x", "adj", "L0_gnn_W1", "L0_gnn_att_src1", "L0_gnn_att_dst1", "L0_gnn_b1", "L0_gnn_W2",
        "L0_gnn_att_src2", "L0_gnn_att_dst2", "L0_gnn_b2", "L1_gnn_attn_w", "L1_gnn_attn_b", "L1_gnn_W1",
        "L1_gnn_b1", "L1_gnn_W2", "L1_gnn_b2", "L1_gnn_g1", "L1_gnn_beta1", "L1_gnn_g2", "L1_gnn_beta2",
        "L2_gnn_attn_w_src", "L2_gnn_attn_w_dst", "L2_gnn_attn_b", "L3_gnn_W", "L3_gnn_attn"]


def kernel(**inputs):
    import numpy as np
    import concourse.bacc as bacc
    from concourse.bass_utils import run_bass_kernel_spmd as run

    nc = bacc.Bacc("TRN2", target_bir_lowering=False, num_devices=1)
    arrays, args = {}, []
    for name in _INS + ["b3_by_part"]:
        a = np.asarray(inputs["L3_gnn_b" if name == "b3_by_part" else name])
        if name == "L1_gnn_b1":
            a = a.reshape(a.shape[0], -1, P).transpose(2, 0, 1)
        if name == "b3_by_part":
            a = a.reshape(-1, P).T
        if name == "L3_gnn_W":
            a = a.T
        a = np.ascontiguousarray(a)
        arrays[f"in_{name}"] = a
        args.append(nc.dram_tensor(f"in_{name}", a.shape, mybir.dt.from_np(a.dtype), kind="ExternalInput").ap())
    out = nc.dram_tensor("out", inputs["x"].shape, F32, kind="ExternalOutput").ap()
    gnn_kernel(nc, *args, out)
    r = run(nc, [arrays], core_ids=[0])
    return r.results[0]["out"]
```
